# Optimizing a Trainium2 kernel written in Bass

```python
import numpy as np
import jax
import jax.numpy as jnp

def _softmax(x, axis=-1):
    return jax.nn.softmax(x, axis=axis)

def _gelu(x):
    return jax.nn.gelu(x, approximate=True)

def _silu(x):
    return jax.nn.silu(x)

def _sigmoid(x):
    return jax.nn.sigmoid(x)

def _layernorm(x, axis=-1, eps=1e-05):
    m = jnp.mean(x, axis=axis, keepdims=True)
    v = jnp.var(x, axis=axis, keepdims=True)
    return (x - m) / jnp.sqrt(v + eps)

def _scatter_add(tgt, idx, src, axis=0):
    return tgt.at[idx].add(src)

def _segment_sum(src, seg, n):
    return jax.ops.segment_sum(src, seg, n)
kernel_name = 'mk_gnn_resnorm_d4_gnn_r32_8bfa0f'

def setup_inputs(seed: int=0):
    np.random.seed(seed)
    _w = jnp.asarray

    def _rec_inputs():
        import jax
        import jax.numpy as jnp
        _gk = jax.random.key(seed)
        x = -0.000202 + 1 * jax.random.normal(jax.random.fold_in(_gk, 1), (3125, 64), jnp.float32)
        _s = jax.random.randint(jax.random.fold_in(_gk, 2), (50000,), 0, 3125, jnp.int32)
        _d = jax.random.randint(jax.random.fold_in(_gk, 3), (50000,), 0, 3125, jnp.int32)
        _loop = jnp.arange(3125, dtype=jnp.int32)
        src = jnp.concatenate([_s, _d, _loop])
        dst = jnp.concatenate([_d, _s, _loop])
        _o = jnp.argsort(dst, stable=True)
        src = src[_o]
        dst = dst[_o]
        edge_attr_32 = 0.000189758 + 1.00013 * jax.random.normal(jax.random.fold_in(_gk, 12), (103125, 32), jnp.float32)
        edge_weight = jax.random.uniform(jax.random.fold_in(_gk, 14), (103125,), jnp.float32, 0.0, 1)
        edge_weight1 = -0.000414295 + 0.999828 * jax.random.normal(jax.random.fold_in(_gk, 15), (103125, 1), jnp.float32)
        return (x, src, dst, edge_attr_32, edge_weight, edge_weight1)
    x, src, dst, edge_attr_32, edge_weight, edge_weight1 = _rec_inputs()

    def _L0_gnn_setup():
        import jax, jax.numpy as jnp
        import numpy as np
        N_NODES = 3125
        N_EDGES = 50000
        IN_FEATS = 64
        OUT_FEATS = 64
        EDGE_FEATS = 1
        key = jax.random.key(seed)
        ks = jax.random.split(key, 6)
        h = jax.random.normal(ks[0], (N_NODES, IN_FEATS), dtype=jnp.float32)
        e = jax.random.normal(ks[1], (N_EDGES, EDGE_FEATS), dtype=jnp.float32)
        src = jax.random.randint(ks[2], (N_EDGES,), 0, N_NODES, dtype=jnp.int32)
        dst = jax.random.randint(ks[3], (N_EDGES,), 0, N_NODES, dtype=jnp.int32)
        cat_dim = 2 * IN_FEATS + EDGE_FEATS
        W1 = jax.random.normal(ks[4], (cat_dim, OUT_FEATS), dtype=jnp.float32) / np.sqrt(cat_dim)
        b1 = jnp.zeros((OUT_FEATS,), dtype=jnp.float32)
        W2 = jax.random.normal(ks[5], (OUT_FEATS, OUT_FEATS), dtype=jnp.float32) / np.sqrt(OUT_FEATS)
        b2 = jnp.zeros((OUT_FEATS,), dtype=jnp.float32)
        return {'h': h, 'e': e, 'src': src, 'dst': dst, 'W1': W1, 'b1': b1, 'W2': W2, 'b2': b2}
    _L0_gnn_all = _L0_gnn_setup()
    _L0_gnn_in = {k: v for k, v in _L0_gnn_all.items() if k in ('W1', 'b1', 'W2', 'b2')}
    del _L0_gnn_all

    def _L1_gnn_setup():
        import jax, jax.numpy as jnp
        import numpy as np
        N, E, D, ED = (3125, 50000, 64, 32)
        LN_EPS = 1e-05
        NEG_SLOPE = 0.2
        key = jax.random.key(seed)
        ks = jax.random.split(key, 12)
        return {'x': jax.random.normal(ks[0], (N, D), jnp.float32), 'edge_index': jax.random.randint(ks[1], (2, E), 0, N, dtype=jnp.int64), 'edge_attr': jax.random.normal(ks[2], (E, ED), jnp.float32), 'We': jax.random.normal(ks[3], (ED, D), jnp.float32) / np.sqrt(ED), 'be': jnp.zeros((D,), jnp.float32), 'W1': jax.random.normal(ks[4], (D, D), jnp.float32) / np.sqrt(D), 'b1': jnp.zeros((D,), jnp.float32), 'W2': jax.random.normal(ks[5], (D, D), jnp.float32) / np.sqrt(D), 'b2': jnp.zeros((D,), jnp.float32), 'eps_gin': jnp.zeros((), jnp.float32), 'gamma': jnp.ones((D,), jnp.float32), 'beta': jnp.zeros((D,), jnp.float32)}
    _L1_gnn_all = _L1_gnn_setup()
    _L1_gnn_in = {k: v for k, v in _L1_gnn_all.items() if k in ('We', 'be', 'W1', 'b1', 'W2', 'b2', 'eps_gin', 'gamma', 'beta')}
    del _L1_gnn_all

    def _L2_gnn_setup():
        import jax, jax.numpy as jnp
        import numpy as np
        N_NODES = 3125
        EMB_DIM = 64
        N_EDGES = 37500
        N_LAYERS = 3
        key = jax.random.key(seed)
        k1, k2, k3 = jax.random.split(key, 3)
        embedding = jax.random.normal(k1, (N_NODES, EMB_DIM), dtype=jnp.float32)
        layer_weights = jnp.ones((N_LAYERS + 1,), dtype=jnp.float32) / (N_LAYERS + 1)
        edge_weight = jax.random.uniform(k2, (N_EDGES,), dtype=jnp.float32)
        edge_index = jax.random.randint(k3, (2, N_EDGES), 0, N_NODES, dtype=jnp.int64)
        return {'embedding': embedding, 'layer_weights': layer_weights, 'edge_weight': edge_weight, 'edge_index': edge_index}
    _L2_gnn_all = _L2_gnn_setup()
    _L2_gnn_in = {k: v for k, v in _L2_gnn_all.items() if k in ('layer_weights',)}
    del _L2_gnn_all

    def _L3_gnn_setup():
        import jax, jax.numpy as jnp
        import numpy as np
        N = 3125
        E = 100000
        D = 64
        K = 10
        ALPHA = 0.1
        key = jax.random.key(seed)
        k1, k2, k3, k4 = jax.random.split(key, 4)
        feat = jax.random.normal(k1, (N, D), dtype=jnp.float32)
        src = jax.random.randint(k2, (E,), 0, N, dtype=jnp.int32)
        dst = jax.random.randint(k3, (E,), 0, N, dtype=jnp.int32)
        edge_weight = jax.random.uniform(k4, (E,), dtype=jnp.float32)
        return {'feat': feat, 'edge_weight': edge_weight, 'src': src, 'dst': dst}
    _L3_gnn_all = _L3_gnn_setup()
    _L3_gnn_in = {k: v for k, v in _L3_gnn_all.items() if k in ()}
    del _L3_gnn_all
    return {'x': x, 'src': src, 'dst': dst, 'edge_attr_32': edge_attr_32, 'edge_weight': edge_weight, 'edge_weight1': edge_weight1, 'L0_gnn_W1': _L0_gnn_in['W1'], 'L0_gnn_b1': _L0_gnn_in['b1'], 'L0_gnn_W2': _L0_gnn_in['W2'], 'L0_gnn_b2': _L0_gnn_in['b2'], 'L1_gnn_We': _L1_gnn_in['We'], 'L1_gnn_be': _L1_gnn_in['be'], 'L1_gnn_W1': _L1_gnn_in['W1'], 'L1_gnn_b1': _L1_gnn_in['b1'], 'L1_gnn_W2': _L1_gnn_in['W2'], 'L1_gnn_b2': _L1_gnn_in['b2'], 'L1_gnn_eps_gin': _L1_gnn_in['eps_gin'], 'L1_gnn_gamma': _L1_gnn_in['gamma'], 'L1_gnn_beta': _L1_gnn_in['beta'], 'L2_gnn_layer_weights': _L2_gnn_in['layer_weights']}

def reference(x, src, dst, edge_attr_32, edge_weight, edge_weight1, L0_gnn_W1, L0_gnn_b1, L0_gnn_W2, L0_gnn_b2, L1_gnn_We, L1_gnn_be, L1_gnn_W1, L1_gnn_b1, L1_gnn_W2, L1_gnn_b2, L1_gnn_eps_gin, L1_gnn_gamma, L1_gnn_beta, L2_gnn_layer_weights):
    import jax
    import jax.numpy as jnp

    def _L0_gnn_ref(h, e, src, dst, W1, b1, W2, b2):
        import jax, jax.numpy as jnp
        import numpy as np
        N_NODES = 3125
        N_EDGES = 50000
        IN_FEATS = 64
        OUT_FEATS = 64
        EDGE_FEATS = 1
        x = jnp.concatenate([h[src], h[dst], e], axis=1)
        m = jax.nn.relu(x @ W1 + b1) @ W2 + b2
        h_new = jax.ops.segment_sum(m, dst, num_segments=h.shape[0])
        return h_new

    def _L1_gnn_ref(x, edge_index, edge_attr, We, be, W1, b1, W2, b2, eps_gin, gamma, beta):
        import jax, jax.numpy as jnp
        import numpy as np
        N, E, D, ED = (3125, 50000, 64, 32)
        LN_EPS = 1e-05
        NEG_SLOPE = 0.2
        src, dst = (edge_index[0], edge_index[1])
        msg = jax.nn.relu(x[src] + edge_attr @ We + be)
        aggr = jax.ops.segment_sum(msg, dst, num_segments=x.shape[0])
        h = (1.0 + eps_gin) * x + aggr
        h = jax.nn.relu(h @ W1 + b1) @ W2 + b2
        h = jnp.where(h >= 0, h, NEG_SLOPE * h)
        mu = jnp.mean(h, axis=-1, keepdims=True)
        var = jnp.mean((h - mu) ** 2, axis=-1, keepdims=True)
        return (h - mu) / jnp.sqrt(var + LN_EPS) * gamma + beta

    def _L2_gnn_ref(embedding, layer_weights, edge_weight, edge_index):
        import jax, jax.numpy as jnp
        import numpy as np
        N_NODES = 3125
        EMB_DIM = 64
        N_EDGES = 37500
        N_LAYERS = 3
        n = embedding.shape[0]
        row, col = (edge_index[0], edge_index[1])
        deg = jax.ops.segment_sum(edge_weight, col, num_segments=n)
        dinv = jnp.where(deg > 0, jax.lax.rsqrt(deg), 0.0)
        norm = dinv[row] * edge_weight * dinv[col]
        x = embedding
        outs = [x]
        for _ in range(N_LAYERS):
            msgs = norm[:, None] * x[row]
            x = jax.ops.segment_sum(msgs, col, num_segments=n)
            outs.append(x)
        w = jax.nn.softmax(layer_weights)
        comb = jnp.einsum('l,lnd->nd', w, jnp.stack(outs))
        nrm = jnp.maximum(jnp.linalg.norm(comb, axis=1, keepdims=True), 1e-12)
        return comb / nrm

    def _L3_gnn_ref(feat, edge_weight, src, dst):
        import jax, jax.numpy as jnp
        import numpy as np
        N = 3125
        E = 100000
        D = 64
        K = 10
        ALPHA = 0.1
        n = feat.shape[0]
        loop = jnp.arange(n, dtype=src.dtype)
        s = jnp.concatenate([src, loop])
        d = jnp.concatenate([dst, loop])
        w = jnp.concatenate([edge_weight, jnp.ones((n,), feat.dtype)])
        deg_out = jax.ops.segment_sum(w, s, num_segments=n)
        deg_in = jax.ops.segment_sum(w, d, num_segments=n)
        inv_sqrt_out = jnp.where(deg_out > 0, jax.lax.rsqrt(deg_out), 0.0)
        inv_sqrt_in = jnp.where(deg_in > 0, jax.lax.rsqrt(deg_in), 0.0)
        wn = w * inv_sqrt_out[s] * inv_sqrt_in[d]
        feat_0 = feat

        def step(h, _):
            agg = jax.ops.segment_sum(h[s] * wn[:, None], d, num_segments=n)
            return ((1.0 - ALPHA) * agg + ALPHA * feat_0, None)
        h, _ = jax.lax.scan(step, feat, None, length=K)
        return h
    edge_index = jnp.stack([src, dst])
    x = _layernorm(x + _L0_gnn_ref(x, edge_weight1, src, dst, L0_gnn_W1, L0_gnn_b1, L0_gnn_W2, L0_gnn_b2), axis=-1)
    x = _layernorm(x + _L1_gnn_ref(x, edge_index, edge_attr_32, L1_gnn_We, L1_gnn_be, L1_gnn_W1, L1_gnn_b1, L1_gnn_W2, L1_gnn_b2, L1_gnn_eps_gin, L1_gnn_gamma, L1_gnn_beta), axis=-1)
    x = _layernorm(x + _L2_gnn_ref(x, L2_gnn_layer_weights, edge_weight, edge_index), axis=-1)
    x = _layernorm(x + _L3_gnn_ref(x, edge_weight, src, dst), axis=-1)
    return x

_drawn_inputs = setup_inputs


def setup_inputs(seed=0):
    import zlib

    import numpy as np

    out = dict(_drawn_inputs(seed))
    spreads = {'L0_gnn_b1': (0.0, 0.1),
     'L0_gnn_b2': (0.0, 0.1),
     'L1_gnn_be': (0.0, 0.1),
     'L1_gnn_b1': (0.0, 2.0),
     'L1_gnn_b2': (0.0, 0.8),
     'L1_gnn_gamma': (1.0, 0.2),
     'L1_gnn_beta': (0.0, 0.1),
     'L2_gnn_layer_weights': (0.25, 0.6)}
    factors = {'edge_weight': 64.0, 'edge_weight1': 8.0}
    for name, (base, spread) in spreads.items():
        noise = np.random.default_rng([zlib.crc32(name.encode()), seed]).standard_normal(out[name].shape)
        drawn = base * np.exp(spread * noise) if base else spread * noise
        out[name] = jnp.asarray(drawn.astype(out[name].dtype))
    for name, factor in factors.items():
        out[name] = (out[name] * factor).astype(out[name].dtype)
    return out
```

```python
from contextlib import ExitStack

import numpy as np

import concourse.bass as bass
from concourse import mybir

N, F, E, ED = 3125, 64, 103125, 32
P = 128
NB = -(-N // P)
NP = NB * P
SBE = 8 * P
NSB = -(-E // SBE)
EP = NSB * SBE
NT = EP // P
WIN = 8
PAIR = 2 * WIN
CH = 512
NCH = N // CH
LASTW = 64
NCOL = NCH * CH + LASTW
NPAIR = NCOL // PAIR
NWIN = 2 * NPAIR
TPW = 4
RES = 9
STR = NB - RES
QC = 128
SPAN = 47
PIECE = 4
NPC = STR // PIECE
RING = 6
WTS = 16 * 10
HALF = 96
EPS = 1e-5
ALPHA = 0.1
K2, K3 = 3, 10
KTOT = K2 + K3
CORDER = [0, NCH] + list(range(1, NCH))
NPOS = NCH + 1
NPIECE = NCH * NPC
TINY = float(np.finfo(np.float32).tiny)

C_FIRST, C_ALL = 13, 17
V_FLD, V_ROWS = 9, 28
NB_Y, NB_X1, NB_WEBD = 5, 12, 15
NC_HT, NC_DEG, NC_LEAKY, NC_X2 = 11, 19, 24, 41
NCT_X1, NCT_H1, NCT_H2, NCT_DEG = 7, 14, 19, 24
NCA_H1, NCA_H2, NCA_ROOT = 7, 12, 13
DEGB = (4, 5, 6, 7, 0)
H2B = (7, 0, 1, 2, 3)
ND_L2, ND_DOUT, ND_LN2, ND_L3, ND_LN3, ND_OUT = 7, 10, 18, 27, 29, 36


class Signals:
    pass


def build(nc, x, src, dst, eattr, ew, ew1, W1_0, b1_0, W2_0, b2_0, We, be, W1_1, b1_1, W2_1, b2_1,
          eps_gin, gamma, beta, lw, out):
    f32, i32 = mybir.dt.float32, mybir.dt.int32
    ALU, ACT, AX = mybir.AluOpType, mybir.ActivationFunctionType, mybir.AxisListType.X
    ds = bass.ds
    ctx = ExitStack()
    with ctx:
        def sem(name):
            return ctx.enter_context(nc.semaphore(name))

        WORDS = 53200
        arena = ctx.enter_context(nc.sbuf_tensor("arena", [P, WORDS], f32))
        top = [0]

        def take(words):
            at = top[0]
            top[0] += words
            assert top[0] <= WORDS, (top[0], WORDS)
            return at

        def at(start, *shape, parts=P, part0=0):
            n = int(np.prod(shape))
            ap = arena[part0:part0 + parts, start:start + n]
            if len(shape) == 2:
                ap = ap.rearrange("p (a b) -> p a b", b=shape[1])
            if len(shape) == 3:
                ap = ap.rearrange("p (a b c) -> p a b c", b=shape[1], c=shape[2])
            return ap

        o_wres = take(RES * NCOL)
        o_w6 = take(STR * LASTW)
        o_iota = take(P)
        o_ident = take(P)
        o_fold = take(HALF)
        o_w1ab = take(P)
        o_w2 = take(HALF)
        o_be = take(F)
        o_hi1 = take(2 * TPW * NB)
        o_small = take(107)
        o_lo = top[0]
        Wres = at(o_wres, RES, NCOL)
        W6 = at(o_w6, STR, LASTW)
        iota = at(o_iota, P)
        ident = at(o_ident, P)
        fold = at(o_fold, HALF)
        w1ab = at(o_w1ab, P)
        w2p = at(o_w2, HALF)
        beB = at(o_be, F)
        hi1 = at(o_hi1, 2 * TPW, NB)
        ones = at(o_small, 1)
        edge8 = at(o_small + 1, 8, parts=NWIN // 4)
        wcols = at(o_small + 9, PAIR)
        wcols0 = at(o_small + 25, PAIR)
        first2 = at(o_small + 105, 2)
        dsel = at(o_small + 41, 2 * TPW, WIN)

        o_xa = take(NB * F)
        o_agg = take(NP)
        o_stage = take(2 * STR * QC)
        o_alo = take(2 * 2 * TPW * P)
        o_outer = take(2 * 2 * TPW * NB * WIN)
        o_rec = take(NT * 4)
        o_g = take(2 * 8 * F)
        o_oh = take(2 * 8 * (SPAN + 1))
        o_oht = take(2 * 4 * P)
        o_qd = take(2 * P)
        o_rel = take(NSB * 8)
        o_ew = take(NSB * 8)
        o_wrec = take(2 * 2 * TPW * 4)
        o_base = take(NSB)
        o_idx = take(2 * 8)
        xa = at(o_xa, NB, F)
        aggT = at(o_agg, NP)
        stage = at(o_stage, 2, STR, QC)
        alo = at(o_alo, 2, 2 * TPW, P)
        outer = at(o_outer, 2, 2 * TPW, NB * WIN)
        rec = at(o_rec, NT, 4)
        G = at(o_g, 2, 8, F)
        OH = at(o_oh, 2, 8, SPAN + 1)
        OHT = at(o_oht, 2, 4 * P, parts=2 * (SPAN + 1))
        QD = at(o_qd, 2, P, parts=2 * (SPAN + 1))
        EA = at(o_oht + 512, 2, 256)
        EAT = at(o_oht, 2, 256)
        WEBD = at(o_qd, 256)
        rel = at(o_rel, NSB * 8)
        ewall = at(o_ew, NSB, 8)
        ewflat = at(o_ew, NSB * 8)
        wrec = at(o_wrec, 2, 2 * TPW, 4)
        base_row = at(o_base, NSB, parts=1).bitcast(i32)
        idx = at(o_idx, 2, 8).bitcast(i32)

        t = [o_wres]

        def tmp(words):
            a = t[0]
            t[0] += words
            assert t[0] <= o_iota
            return a
        dstN = at(tmp(SBE), SBE, parts=NSB).bitcast(i32)
        srcN = at(tmp(SBE), SBE, parts=NSB).bitcast(i32)
        fld = [at(tmp(SBE), SBE, parts=NSB) for _ in range(4)]
        srcI = [at(tmp(SBE), SBE, parts=NSB).bitcast(i32) for _ in range(2)]
        o_tm = tmp(NSB * 17)
        tmin = at(o_tm, NSB * 0 + 8, parts=NSB)
        tmax = at(o_tm + 8, 8, parts=NSB)
        bmin = at(o_tm + 16, 1, parts=NSB)
        tminB = at(tmp(NT), NT)
        tmaxB = at(tmp(NT), NT)
        bB = at(tmp(NSB), NSB)
        WQ = NWIN // 4
        c1 = at(tmp(NT), NT, parts=WQ)
        c2 = at(tmp(NT), NT, parts=WQ)
        tiota = at(tmp(NT), NT)
        lohi = at(tmp(32), 32, parts=WQ)
        lo_i = lohi[:, 8:12].bitcast(i32)
        dstS = at(tmp(NSB * 8), NSB, 8).bitcast(i32)
        PQ = at(tmp(NB * P), NB, P)
        xT = at(tmp(NP), NP)

        lnA = at(o_outer, NB, F)
        lnB = at(o_alo, NB, F)
        lnS = at(o_outer + NB * F, 8, NB)
        hT = at(o_stage, NP)
        h1T = at(o_rec, NP)
        o_l1 = o_g
        w1n = at(o_l1, F, parts=F)
        w2n = at(o_l1 + F, HALF, parts=F + 1)
        b1n = at(o_l1 + F + HALF, 1, parts=F)
        epsn = at(o_l1 + F + HALF + 1, 1)
        gam = at(o_l1 + F + HALF + 2, F)
        bet = at(o_l1 + 2 * F + HALF + 2, F)
        sel = at(o_l1 + 3 * F + HALF + 2, HALF)

        top[0] = o_lo
        x2 = at(take(NB * F), NB, F)
        assert o_lo == o_xa
        o_ring = take(RING * PIECE * CH)
        ring = at(o_ring, RING, PIECE * CH)
        xs = [at(take(NB * F), NB, F) for _ in range(2)]
        comb = at(take(NB * F), NB, F)
        gb = at(take(NB * F), NB, F)
        accS = at(take(3 * CH), 3, CH)
        accL = at(take(P), P)
        post = at(take(4 * F), 4, F)
        nsc = at(take(12 * NB), 12, NB)
        lwt = at(take(16), 16)
        deg_str = at(take((NCH + 1) * STR), NCH + 1, STR)

        banks = [ctx.enter_context(nc.psum_tensor(f"bank{i}", [P, CH], f32)) for i in range(8)]
        psW = [banks[0][:, 0:NB * PAIR], banks[1][:, 0:NB * PAIR]]
        psPre = [banks[2], banks[3]]
        psT = banks[4]
        psSeg = banks[5]

        def dram(name, shape, dt=f32):
            return nc.dram_tensor(name, shape, dt, kind="Internal").ap()
        d_p = dram("d_p", [NP, F])
        d_q = dram("d_q", [NP, F])
        d_t1 = dram("d_t1", [NP, F])
        d_tmin = dram("d_tmin", [NT])
        d_tmax = dram("d_tmax", [NT])
        d_bmin = dram("d_bmin", [NSB])
        d_base = dram("d_base", [1, NSB], i32)
        d_lo = dram("d_lo", [1, NWIN], i32)
        d_w = dram("d_w", [P, NCH * CH // QC, STR, QC])

        def two(name):
            return [sem(name + "_0"), sem(name + "_1")]
        s = Signals()
        s.consts = sem("consts")
        s.ld_edges = sem("ld_edges")
        s.ld_sb = sem("ld_sb")
        s.ld_x = sem("ld_x")
        s.ld_wts = sem("ld_wts")
        s.ld_bc = sem("ld_bc")
        s.st_min = sem("st_min")
        s.st_rows = sem("st_rows")
        s.st_pq = sem("st_pq")
        s.prep_v = sem("prep_v")
        s.rec_t = sem("rec_t")
        s.rec_c = sem("rec_c")
        s.xt_t = sem("xt_t")
        s.xt_c = sem("xt_c")
        s.pq_t = sem("pq_t")
        s.pq_c = sem("pq_c")
        s.wrec = two("wrec")
        s.pair_step = sem("pair_step")
        s.pair_v = two("pair_v")
        s.pair_t = two("pair_t")
        s.pair_e = two("pair_e")
        s.deg_v = sem("deg_v")
        s.stg = two("stg")
        s.nb_v = sem("nb_v")
        s.nb_a = sem("nb_a")
        s.nb_t = sem("nb_t")
        s.st_t1 = sem("st_t1")
        s.ld_w = sem("ld_w")
        s.ld_we = sem("ld_we")
        s.nc_v = sem("nc_v")
        s.nc_a = sem("nc_a")
        s.nc_t = sem("nc_t")
        s.ld_l1 = sem("ld_l1")
        s.ld_lw = sem("ld_lw")
        s.pc = [sem(f"pc{i}") for i in range(RING)]
        s.pc_free = sem("pc_free")
        s.acc_t = sem("acc_t")
        s.acc_c = sem("acc_c")
        s.out_t = sem("out_t")
        s.post_v = sem("post_v")
        s.xs_v = sem("xs_v")
        s.nd_v = sem("nd_v")
        s.nd_a = sem("nd_a")
        s.st_out = sem("st_out")

        def layer_signals(layer):
            r = Signals()
            r.idx = two(f"idx{layer}")
            r.qd = two(f"qd{layer}")
            r.g = two(f"g{layer}")
            r.oh = two(f"oh{layer}")
            r.tr = two(f"tr{layer}")
            r.trc = two(f"trc{layer}")
            r.pre = two(f"pre{layer}")
            r.add = two(f"add{layer}")
            r.relu = two(f"relu{layer}")
            r.seg = two(f"seg{layer}")
            r.agg = two(f"agg{layer}")
            r.ea = two(f"ea{layer}")
            return r
        R = [layer_signals(0), layer_signals(1)]

        block = ctx.enter_context(nc.Block())

        NLOOP = NCH // 2 * CH // PAIR
        NQ = NCH * CH // QC

        def edge_loop(eng, layer, superblock, quarter_end=None):
            r = R[layer]
            with eng.Fori(0, NLOOP // 16) as u:
                for q in range(2):
                    with eng.Fori(0, 4) as m:
                        for b in range(2):
                            h = 8 * u + 4 * q + m
                            kh = h + layer * (NLOOP // 2)
                            superblock(r, 2 * h + b, h, b, 2 * kh + b, kh, q, 2 * m + b, u + layer * (NLOOP // 16), True)
                    if quarter_end:
                        quarter_end(2 * u + q + layer * (NLOOP // 8), q, u + layer * (NLOOP // 16))
            for i in range(NLOOP, NSB):
                k = i + NLOOP
                if layer == 0 or k >= NPAIR:
                    k = None
                superblock(r, i, i // 2, i % 2, k, None if k is None else k // 2, None, i - NLOOP, None, i + 1 < NSB)
            if layer == 1 and quarter_end:
                quarter_end(NQ, None, None)

        def following(h, b):
            return (h, 1) if b == 0 else (h + 1, 0)

        def rows(t, i):
            return t.rearrange("(i p k) -> i p k", p=P, k=8)[ds(i, 1), :, :].rearrange("o p k -> p (o k)")

        def start_rings(eng, names):
            for x in names:
                for each in x:
                    eng.sem_inc(each, 1)

        @block.sync
        def _(sp):
            sp.dma_start(dstN, dst.rearrange("(p e) -> p e", e=SBE)).then_inc(s.ld_edges, 16)
            sp.dma_start(srcN, src.rearrange("(p e) -> p e", e=SBE)).then_inc(s.ld_edges, 16)
            sp.dma_start(fld[3], ew.rearrange("(p e) -> p e", e=SBE)).then_inc(s.ld_edges, 16)
            sp.dma_start(dstS, dst.rearrange("(i p k) -> p i k", p=P, k=8)).then_inc(s.ld_sb, 16)
            sp.dma_start(ewall, ew1.rearrange("(i p k) -> p i k", p=P, k=8)).then_inc(s.ld_sb, 16)
            sp.wait_ge(s.prep_v, 5)
            sp.dma_start(d_tmin.rearrange("(p k) -> p k", k=8), tmin).then_inc(s.st_min, 16)
            sp.dma_start(d_tmax.rearrange("(p k) -> p k", k=8), tmax).then_inc(s.st_min, 16)
            sp.dma_start(d_bmin.rearrange("(p k) -> p k", k=1), bmin).then_inc(s.st_min, 16)
            sp.wait_ge(s.st_min, 48)
            sp.dma_start(bB, d_bmin.rearrange("(o k) -> o k", o=1).to_broadcast([P, NSB])).then_inc(s.ld_bc, 16)
            sp.dma_start(tminB, d_tmin.rearrange("(o k) -> o k", o=1).to_broadcast([P, NT])).then_inc(s.ld_bc, 16)
            sp.dma_start(tmaxB, d_tmax.rearrange("(o k) -> o k", o=1).to_broadcast([P, NT])).then_inc(s.ld_bc, 16)
            sp.wait_ge(s.pq_c, 7)
            sp.dma_start(d_p.rearrange("(a p) f -> p a f", p=P), PQ[:, :, 0:F]).then_inc(s.st_pq, 16)
            sp.dma_start(d_q.rearrange("(a p) f -> p a f", p=P), PQ[:, :, F:P]).then_inc(s.st_pq, 16)
            sp.wait_ge(s.prep_v, V_ROWS)
            sp.dma_start(d_base, base_row).then_inc(s.st_rows, 16)
            sp.dma_start(d_lo.rearrange("o (p k) -> p (o k)", k=4), lo_i).then_inc(s.st_rows, 16)
            sp.wait_ge(s.st_rows, 32)
            sp.wait_ge(s.st_pq, 32)
            sp.wait_ge(s.rec_c, 8)

            def superblock(r, i, h, b, k, kh, q, mb, qh, more):
                sp.wait_ge(r.add[b], h + 1)
                sp.dma_start(idx[:, b, :], rows(src, i)).then_inc(r.idx[b], 16)
                if r is R[0]:
                    base = sp.value_load(d_base[0:1, ds(i, 1)], min_val=0, max_val=N - 1)
                    sp.wait_ge(r.pre[b], h + 1)
                    for half in range(2):
                        sp.dma_start(QD[(SPAN + 1) * half:(SPAN + 1) * half + SPAN, b, F * half:F * half + F],
                                     d_q[ds(base, SPAN), :]).then_inc(r.qd[b], 16)
                else:
                    sp.wait_ge(r.tr[b], h + 1)
                    sp.dma_start(EA[:, b, :], eattr.rearrange("(i p k) f -> i p (k f)", p=P, k=8)[ds(i, 1), :, :]
                                 .rearrange("o p e -> p (o e)")).then_inc(r.ea[b], 16)
                if k is not None:
                    for w in range(2):
                        lo = sp.value_load(d_lo[0:1, ds(2 * k + w, 1)], min_val=0, max_val=NT - TPW)
                        if w == 0:
                            sp.wait_ge(s.pair_v[b], kh + 1)
                        sp.dma_start(wrec[:, b, w * TPW:(w + 1) * TPW, :],
                                     rec[:, ds(lo, TPW), :]).then_inc(s.wrec[b], 16)

            edge_loop(sp, 0, superblock)
            sp.wait_ge(R[0].oh[0], 2 * (NSB // 2 + 1))
            sp.wait_ge(R[0].oh[1], 2 * (NSB // 2))
            sp.dma_start(ewall, ew.rearrange("(i p k) -> p i k", p=P, k=8)).then_inc(s.ld_w, 16)
            sp.wait_ge(R[0].pre[0], NSB // 2 + 1 + 1)
            sp.wait_ge(s.nb_v, NB_WEBD)
            for j in range(4):
                sp.dma_start(WEBD[ED * j:ED * j + ED, F * j:F * j + F], We).then_inc(s.ld_we, 16)
            edge_loop(sp, 1, superblock)
            sp.wait_ge(R[1].agg[0], NSB // 2 + 1 + 1)
            sp.wait_ge(R[1].agg[1], NSB // 2 + 1)
            sp.wait_ge(s.nc_v, 1)
            for o, i_ in ((w1n, W1_1), (w2n[0:F, 0:F], W2_1), (w2n[F:F + 1, 0:F], b2_1.rearrange("(o f) -> o f", o=1)),
                          (b1n, b1_1.rearrange("(f o) -> f o", o=1)),
                          (epsn, eps_gin.rearrange("(o k) -> o k", o=1).to_broadcast([P, 1])),
                          (gam, gamma.rearrange("(o f) -> o f", o=1).to_broadcast([P, F])),
                          (bet, beta.rearrange("(o f) -> o f", o=1).to_broadcast([P, F]))):
                sp.dma_start(o, i_).then_inc(s.ld_l1, 16)
            sp.wait_ge(s.stg[0], 16 * (NQ // 2) + 16)
            sp.wait_ge(s.stg[1], 16 * (NQ // 2) + 16)
            sp.wait_ge(s.nc_v, NC_X2)

            def load_piece(j):
                c, part = j // NPC, j % NPC
                sp.dma_start(ring[:, j % RING, :].rearrange("p (q e) -> p q e", q=CH // QC),
                             d_w[:, c * (CH // QC):(c + 1) * (CH // QC), part * PIECE:(part + 1) * PIECE, :]
                             .rearrange("p q a e -> p q (a e)")).then_inc(s.pc[j % RING], 16)

            def piece_used(k, j):
                c, part = j // NPC, j % NPC
                if part == NPC - 1:
                    sp.wait_ge(s.acc_t, NPOS * k + CORDER.index(c) + 1)
                else:
                    sp.wait_ge(s.pc_free, (NPC - 1) * (NCH * k + c) + part + 1)
            for j in range(RING):
                load_piece(j)
            for j in range(NPIECE):
                piece_used(0, j)
                sp.wait_ge(s.deg_v, j + 1 + (j >= NPC))
                load_piece((j + RING) % NPIECE)
            with sp.Fori(1, KTOT - 1) as k:
                for j in range(NPIECE):
                    piece_used(k, j)
                    load_piece((j + RING) % NPIECE)
            for j in range(NPIECE - RING):
                piece_used(KTOT - 1, j)
                load_piece(j + RING)
            sp.wait_ge(s.nd_v, ND_OUT)
            sp.dma_start(out[0:(NB - 1) * P, :].rearrange("(a p) f -> p a f", p=P), xs[0][:, 0:NB - 1, :]).then_inc(s.st_out, 16)
            sp.dma_start(out[(NB - 1) * P:N, :], xs[0][0:N - (NB - 1) * P, NB - 1, :]).then_inc(s.st_out, 16)
            sp.wait_ge(s.st_out, 32)

        @block.gpsimd
        def _(pool):
            g = nc.gpsimd
            g.iota(iota, pattern=[[1, P]], base=0, channel_multiplier=0, allow_small_or_imprecise_dtypes=True).then_inc(s.consts, 1)
            g.iota(tiota, pattern=[[1, NT]], base=0, channel_multiplier=0, allow_small_or_imprecise_dtypes=True).then_inc(s.consts, 1)
            g.iota(edge8[:, 0:4], pattern=[[WIN, 4]], base=0, channel_multiplier=4 * WIN, allow_small_or_imprecise_dtypes=True).then_inc(s.consts, 1)
            g.iota(edge8[:, 4:8], pattern=[[WIN, 4]], base=WIN - 1, channel_multiplier=4 * WIN, allow_small_or_imprecise_dtypes=True).then_inc(s.consts, 1)
            g.memset(ident, 0.0).then_inc(s.consts, 1)
            g.memset(fold, 0.0).then_inc(s.consts, 1)
            g.memset(at(o_qd, 2, P), 0.0).then_inc(s.consts, 1)
            g.memset(aggT, 0.0).then_inc(s.consts, 1)
            g.memset(ones, 1.0).then_inc(s.consts, 1)
            g.iota(wcols0, pattern=[[1, PAIR]], base=-PAIR, channel_multiplier=0, allow_small_or_imprecise_dtypes=True).then_inc(s.consts, 1)
            pool.wait_ge(s.consts, C_FIRST)
            g.affine_select(out=ident, in_=ident, compare_op=ALU.not_equal, fill=1.0, base=0,
                            pattern=[[-1, P]], channel_multiplier=1).then_inc(s.consts, 1)
            g.affine_select(out=fold, in_=fold, compare_op=ALU.not_equal, fill=1.0, base=0,
                            pattern=[[-1, HALF]], channel_multiplier=1).then_inc(s.consts, 1)
            pool.wait_ge(s.consts, C_FIRST + 2)
            g.affine_select(out=fold[:, 0:F], in_=fold[:, 0:F], compare_op=ALU.not_equal, fill=1.0, base=-F,
                            pattern=[[-1, F]], channel_multiplier=1).then_inc(s.consts, 1)
            pool.wait_ge(s.consts, C_FIRST + 3)
            g.memset(fold[:, F:HALF], 0.0).then_inc(s.consts, 1)

            def superblock(r, i, h, b, k, kh, q, mb, qh, more):
                table = d_p if r is R[0] else d_t1
                pool.wait_ge(r.idx[b], 16 * (h + 1))
                pool.wait_ge(r.seg[b], h + 1)
                pool.nop(nofuse=True)
                for j in range(8):
                    g.indirect_dma_start(G[:, b, j, :], None, table,
                                         bass.IndirectOffsetOnAxis(ap=idx[:, b, j:j + 1], axis=0)).then_inc(r.g[b], 16)

            pool.wait_ge(s.st_pq, 32)
            edge_loop(pool, 0, superblock)
            pool.wait_ge(s.st_t1, 16)
            edge_loop(pool, 1, superblock)

        @block.vector
        def _(v):
            d = nc.vector
            start_rings(v, [s.pair_v, [s.pair_step]] + [x for r in R for x in (r.agg, r.add)])
            V_IN = [0]

            def prep(ins):
                V_IN[0] += 1
                ins.then_inc(s.prep_v, 1)
                v.wait_ge(s.prep_v, V_IN[0])
            d.memset(xT[F:F + 1, :], 1.0).then_inc(s.consts, 1)
            d.memset(w1ab, 0.0).then_inc(s.consts, 1)
            d.memset(w2p, 0.0).then_inc(s.consts, 1)
            v.wait_ge(s.ld_edges, 48)
            prep(d.tensor_copy(fld[2], dstN))
            prep(d.tensor_reduce(tmin, fld[2].rearrange("p (k e) -> p k e", e=P), AX, ALU.min))
            prep(d.tensor_reduce(tmax, fld[2].rearrange("p (k e) -> p k e", e=P), AX, ALU.max))
            prep(d.tensor_scalar(tmax, tmax, float(N - 1), None, ALU.min))
            prep(d.tensor_reduce(bmin, tmin, AX, ALU.min))
            prep(d.tensor_scalar(srcI[0], srcN, P - 1, None, ALU.bitwise_and))
            prep(d.tensor_scalar(srcI[1], srcN, 7, None, ALU.logical_shift_right))
            prep(d.tensor_copy(fld[0], srcI[0]))
            prep(d.tensor_copy(fld[1], srcI[1]))
            assert V_IN[0] == V_FLD
            v.wait_ge(s.ld_bc, 48)
            v.wait_ge(s.ld_sb, 32)
            prep(d.tensor_copy(base_row, bB[0:1, :]))
            prep(d.tensor_tensor(rel.rearrange("p (i k) -> p i k", k=8), dstS, bB.unsqueeze(2).to_broadcast([P, NSB, 8]), ALU.subtract))
            v.wait_ge(s.consts, C_FIRST)
            for q in range(4):
                prep(d.tensor_scalar(c1, tminB[0:WQ, :], edge8[:, 4 + q:5 + q], None, ALU.is_le))
                prep(d.scalar_tensor_tensor(c1, tmaxB[0:WQ, :], edge8[:, q:q + 1], c1, ALU.is_ge, ALU.mult))
                prep(d.scalar_tensor_tensor(c2, c1, -4096.0, tiota[0:WQ, :], ALU.mult, ALU.add))
                prep(d.tensor_reduce(lohi[:, q:q + 1], c2, AX, ALU.min))
            prep(d.tensor_scalar(lo_i, lohi[:, 0:4], 4096.0, float(NT - TPW), ALU.add, ALU.min))
            assert V_IN[0] == V_ROWS

            v.wait_ge(s.consts, C_ALL)

            def one_hots(r, i, h, b):
                v.wait_ge(r.seg[b], h + 1)
                d.tensor_tensor(OH[:, b, :, 0:SPAN],
                                rel[:, ds(8 * i, 8)].unsqueeze(2).to_broadcast([P, 8, SPAN]),
                                iota[:, 0:SPAN].unsqueeze(1).to_broadcast([P, 8, SPAN]), ALU.is_equal).then_inc(r.oh[b], 1)
                d.tensor_copy(OH[:, b][:, :, SPAN:SPAN + 1],
                              ewflat[:, ds(8 * i, 8)].unsqueeze(2)).then_inc(r.oh[b], 1)

            def pair(k, kh, b):
                v.wait_ge(s.wrec[b], 32 * (kh + 1))
                v.wait_ge(s.pair_t[b], kh + 1)
                w_ = wrec[:, b]
                bc = lambda f, n: w_[:, :, f:f + 1].to_broadcast([P, 2 * TPW, n])
                hp, bp = following(kh, b)
                v.wait_ge(s.pair_v[bp], hp + 1)
                v.wait_ge(s.pair_step, 5 * k + 1)
                d.tensor_scalar(wcols, wcols, float(PAIR), None, ALU.add).then_inc(s.pair_step, 1)
                d.tensor_tensor(alo[:, b], bc(0, P), iota.unsqueeze(1).to_broadcast([P, 2 * TPW, P]), ALU.is_equal).then_inc(s.pair_step, 1)
                d.tensor_tensor(hi1, bc(1, NB), iota[:, 0:NB].unsqueeze(1).to_broadcast([P, 2 * TPW, NB]), ALU.is_equal).then_inc(s.pair_step, 1)
                v.wait_ge(s.pair_step, 5 * k + 1 + 1)
                d.tensor_tensor(dsel.rearrange("p (w t) j -> p w t j", w=2),
                                w_[:, :, 2:3].rearrange("p (w t) o -> p w t o", w=2).to_broadcast([P, 2, TPW, WIN]),
                                wcols.rearrange("p (w j) -> p w j", w=2).unsqueeze(2).to_broadcast([P, 2, TPW, WIN]),
                                ALU.is_equal).then_inc(s.pair_step, 1)
                v.wait_ge(s.pair_step, 5 * k + 4 + 1)
                d.tensor_tensor(dsel, dsel, bc(3, WIN), ALU.mult).then_inc(s.pair_step, 1)
                v.wait_ge(s.pair_step, 5 * k + 5 + 1)
                d.tensor_tensor(outer[:, b].rearrange("p t (c j) -> p t c j", j=WIN),
                                hi1.unsqueeze(3).to_broadcast([P, 2 * TPW, NB, WIN]),
                                dsel.unsqueeze(2).to_broadcast([P, 2 * TPW, NB, WIN]), ALU.mult).then_inc(s.pair_v[b], 1)

            def superblock(r, i, h, b, k, kh, q, mb, qh, more):
                base = v.value_load(base_row[0:1, ds(i, 1)], min_val=0, max_val=N - 1)
                v.wait_ge(r.pre[b], h + 1 + 1)
                v.wait_ge(r.g[b], P * (h + 1))
                gflat = G[:, b].rearrange("p k f -> p (k f)")
                d.tensor_tensor(gflat, psPre[b][:, :], gflat, ALU.add).then_inc(r.add[b], 1)
                hn, bn = following(h, b)
                if more:
                    one_hots(r, i + 1, hn, bn)
                if k is not None:
                    pair(k, kh, b)
                v.wait_ge(r.seg[b], h + 1 + 1)
                v.wait_ge(r.agg[bn], hn + 1)
                cols = aggT[:, ds(base, SPAN)]
                d.tensor_tensor(cols, psSeg[:, P * b:P * b + SPAN], cols, ALU.add).then_inc(r.agg[b], 1)

            d.tensor_copy(wcols, wcols0).then_inc(s.prep_v, 1)
            v.wait_ge(s.prep_v, V_ROWS + 1)
            one_hots(R[0], 0, 0, 0)
            edge_loop(v, 0, superblock)

            cnt = [0]

            def link(ins, name=None):
                cnt[0] += 1
                ins.then_inc(s.nb_v, 1)
                v.wait_ge(s.nb_v, cnt[0])

            def norm(link_, a_sem, a_at, y, tmp_, sc, out_):
                link_(d.tensor_reduce(sc[:, 0, :], y, AX, ALU.add))
                link_(d.tensor_scalar(sc[:, 1, :], sc[:, 0, :], -1.0 / F, None, ALU.mult))
                link_(d.tensor_tensor(y, y, sc[:, 1, :].unsqueeze(2).to_broadcast([P, NB, F]), ALU.add))
                v.wait_ge(a_sem, a_at)
                link_(d.tensor_reduce(sc[:, 2, :], tmp_, AX, ALU.add))
                link_(d.tensor_scalar(sc[:, 3, :], sc[:, 2, :], 1.0 / F, EPS, ALU.mult, ALU.add))
                v.wait_ge(a_sem, a_at + 1)
                link_(d.reciprocal(sc[:, 5, :], sc[:, 4, :]))
                link_(d.tensor_tensor(out_, y, sc[:, 5, :].unsqueeze(2).to_broadcast([P, NB, F]), ALU.mult))

            for g5 in range(5):
                v.wait_ge(s.nb_t, g5 + 1)
                link(d.tensor_tensor(lnA[:, 5 * g5:5 * g5 + 5, :], banks[g5][:, 0:5 * HALF].rearrange("p (a c) -> p a c", c=HALF)[:, :, 0:F],
                                     xa[:, 5 * g5:5 * g5 + 5, :], ALU.add))
            norm(link, s.nb_a, 1, lnA, lnB, lnS, xa)
            v.wait_ge(s.ld_wts, WTS)
            assert cnt[0] == NB_X1
            link(d.tensor_tensor(lnB, xa, beB.unsqueeze(1).to_broadcast([P, NB, F]), ALU.add))
            link(d.memset(aggT, 0.0))
            link(d.memset(WEBD, 0.0))
            assert cnt[0] == NB_WEBD
            v.wait_ge(s.ld_w, 16)
            v.wait_ge(s.st_t1, 16)
            one_hots(R[1], 0, 0, 0)
            edge_loop(v, 1, superblock)

            cnt[0] = 0

            def link2(ins):
                cnt[0] += 1
                ins.then_inc(s.nc_v, 1)
                v.wait_ge(s.nc_v, cnt[0])
            link2(d.memset(at(o_l1, 4 * F + 3 * HALF), 0.0))
            v.wait_ge(s.ld_l1, 7 * 16)
            link2(d.tensor_scalar(epsn, epsn, 1.0, None, ALU.add))
            link2(d.memset(sel[F:F + 1, 0:1], 1.0))
            link2(d.memset(h1T[F:F + 1, :], 1.0))
            v.wait_ge(s.stg[0], 16 * (NQ // 2) + 16)
            v.wait_ge(s.stg[1], 16 * (NQ // 2) + 16)
            for g4 in range(7):
                w_ = min(CH, NP - CH * g4)
                v.wait_ge(s.nc_t, g4 + 1)
                link2(d.scalar_tensor_tensor(hT[0:F, CH * g4:CH * g4 + w_], banks[g4][0:F, 0:w_], epsn[0:F, :],
                                             aggT[0:F, CH * g4:CH * g4 + w_], ALU.mult, ALU.add))
            assert cnt[0] == NC_HT
            v.wait_ge(s.nc_t, NCT_DEG)
            for g5 in range(5):
                link2(d.tensor_copy(nsc[:, 0, 5 * g5:5 * g5 + 5],
                                    banks[DEGB[g5]][:, 0:5 * HALF].rearrange("p (a c) -> p a c", c=HALF)[:, :, 0]))
            link2(d.tensor_scalar(nsc[:, 2, :], nsc[:, 0, :], 1.0, None, ALU.add))
            link2(d.tensor_scalar(nsc[:, 4, :], nsc[:, 0, :], TINY, None, ALU.max))
            link2(d.tensor_scalar(nsc[:, 5, :], nsc[:, 2, :], TINY, None, ALU.max))
            assert cnt[0] == NC_DEG
            v.wait_ge(s.nc_a, NCA_ROOT)
            link2(d.reciprocal(nsc[:, 4:6, :], nsc[:, 7:9, :]))
            link2(d.scalar_tensor_tensor(nsc[:, 7, :], nsc[:, 0, :], 0.0, nsc[:, 4, :], ALU.is_gt, ALU.mult))
            link2(d.scalar_tensor_tensor(nsc[:, 8, :], nsc[:, 2, :], 0.0, nsc[:, 5, :], ALU.is_gt, ALU.mult))
            link2(d.tensor_scalar(nsc[:, 10, :], nsc[:, 8, :], 1.0 - ALPHA, None, ALU.mult))
            dinv, dout, a_last, a_mid = nsc[:, 7, :], nsc[:, 9, :], nsc[:, 10, :], nsc[:, 11, :]
            v.wait_ge(s.nc_a, NCA_H2)
            link2(d.scalar_tensor_tensor(lnA, lnA, 0.2, lnA, ALU.mult, ALU.max))
            assert cnt[0] == NC_LEAKY
            norm(link2, s.nc_a, NCA_ROOT + 1, lnA, lnB, lnS, lnB)
            link2(d.tensor_tensor(lnB, lnB, gam.unsqueeze(1).to_broadcast([P, NB, F]), ALU.mult))
            link2(d.tensor_tensor(lnB, lnB, bet.unsqueeze(1).to_broadcast([P, NB, F]), ALU.add))
            link2(d.tensor_tensor(lnA, lnB, xa, ALU.add))
            norm(link2, s.nc_a, NCA_ROOT + 3, lnA, lnB, lnS, x2)
            assert cnt[0] == NC_X2, cnt[0]
            v.wait_ge(s.ld_lw, 16)

            cnt[0] = 0

            def link3(ins):
                cnt[0] += 1
                ins.then_inc(s.nd_v, 1)
                v.wait_ge(s.nd_v, cnt[0])

            def by_node(col, lo_=0, n=NB):
                return col[:, lo_:lo_ + n].unsqueeze(2).to_broadcast([P, n, F])
            link3(d.tensor_tensor(xs[0], x2, by_node(dinv), ALU.mult))
            link3(d.tensor_reduce(lwt[:, 4:5], lwt[:, 0:4], AX, ALU.max))
            link3(d.tensor_scalar(lwt[:, 5:6], lwt[:, 4:5], -1.0, None, ALU.mult))
            v.wait_ge(s.nd_a, 1)
            link3(d.tensor_reduce(lwt[:, 10:11], lwt[:, 6:10], AX, ALU.add))
            link3(d.reciprocal(lwt[:, 11:12], lwt[:, 10:11]))
            link3(d.tensor_scalar(lwt[:, 12:16], lwt[:, 6:10], lwt[:, 11:12], None, ALU.mult))
            link3(d.tensor_scalar(comb.rearrange("p a f -> p (a f)"), x2.rearrange("p a f -> p (a f)"), lwt[:, 12:13], None, ALU.mult))
            assert cnt[0] == ND_L2

            def sums(k, c):
                if not isinstance(k, int):
                    return
                if k == 0 and c == NCH:
                    d.tensor_reduce(deg_str[:, c, :], W6, AX, ALU.add).then_inc(s.deg_v, 1)
                elif k == 0:
                    for j in range(NPC * c, NPC * c + NPC):
                        v.wait_ge(s.pc[j % RING], 16 * (j // RING + 1))
                        part = (j % NPC) * PIECE
                        d.tensor_reduce(deg_str[:, c, part:part + PIECE],
                                        ring[:, j % RING, :].rearrange("p (q a e) -> p a q e", q=CH // QC, e=QC),
                                        mybir.AxisListType.XY, ALU.add).then_inc(s.deg_v, 1)
                elif k == 1:
                    for n in range(RES * CORDER.index(c) // NPOS, RES * (CORDER.index(c) + 1) // NPOS):
                        d.tensor_reduce(nsc[:, 1, n:n + 1], Wres[:, n, :], AX, ALU.add).then_inc(s.deg_v, 1)

            def post_chunks(k, old, new, steps):
                for t_, c in enumerate(CORDER):
                    n = 4 if c < NCH else 1
                    lo_ = 4 * c
                    sums(k, c)
                    v.wait_ge(s.out_t, NPOS * k + t_ + 1)
                    prod = banks[4 + t_ % 4][:, 0:n * HALF].rearrange("p (a c) -> p a c", c=HALF)[:, :, 0:F]
                    steps(k, t_, lo_, n, prod, old, new)

            def step2(k, t_, lo_, n, prod, old, new):
                y = post[:, 0:n, :]
                if t_ or not isinstance(k, int) or k:
                    v.wait_ge(s.xs_v, NPOS * k + t_)
                d.tensor_tensor(y, prod, by_node(dinv, lo_, n), ALU.mult).then_inc(s.post_v, 1)
                v.wait_ge(s.post_v, 2 * (NPOS * k + t_) + 1)
                cb = comb[:, lo_:lo_ + n, :]
                d.scalar_tensor_tensor(cb, y, lwt[:, 13 + k:14 + k], cb, ALU.mult, ALU.add).then_inc(s.post_v, 1)
                v.wait_ge(s.post_v, 2 * (NPOS * k + t_) + 2)
                d.tensor_tensor(new[:, lo_:lo_ + n, :], y, by_node(dinv, lo_, n), ALU.mult).then_inc(s.xs_v, 1)

            def step3(a):
                def step(k, t_, lo_, n, prod, old, new):
                    y = post[:, 0:n, :]
                    v.wait_ge(s.xs_v, NPOS * k + t_)
                    d.tensor_tensor(y, prod, old[:, lo_:lo_ + n, :], ALU.add).then_inc(s.post_v, 1)
                    v.wait_ge(s.post_v, 2 * (NPOS * k + t_) + 1)
                    d.tensor_tensor(y, y, by_node(a, lo_, n), ALU.mult).then_inc(s.post_v, 1)
                    v.wait_ge(s.post_v, 2 * (NPOS * k + t_) + 2)
                    d.tensor_tensor(new[:, lo_:lo_ + n, :], y, gb[:, lo_:lo_ + n, :], ALU.add).then_inc(s.xs_v, 1)
                return step

            for k in range(K2):
                post_chunks(k, xs[k % 2], xs[(k + 1) % 2], step2)
            v.wait_ge(s.xs_v, NPOS * K2)
            v.wait_ge(s.deg_v, NPIECE + 1 + RES)
            link3(d.tensor_reduce(nsc[:, 1, RES:NB], deg_str.rearrange("p c n -> p n c"), AX, ALU.add))
            link3(d.tensor_scalar(nsc[:, 3, :], nsc[:, 1, :], 1.0, None, ALU.add))
            link3(d.tensor_scalar(nsc[:, 6, :], nsc[:, 3, :], TINY, None, ALU.max))
            assert cnt[0] == ND_DOUT
            v.wait_ge(s.nd_a, 3)
            link3(d.reciprocal(nsc[:, 6, :], nsc[:, 9, :]))
            link3(d.scalar_tensor_tensor(nsc[:, 9, :], nsc[:, 3, :], 0.0, nsc[:, 6, :], ALU.is_gt, ALU.mult))
            link3(d.tensor_tensor(nsc[:, 11, :], nsc[:, 10, :], nsc[:, 9, :], ALU.mult))
            link3(d.tensor_reduce(nsc[:, 0, :], gb, AX, ALU.add))
            v.wait_ge(s.nd_a, 4)
            link3(d.tensor_scalar(nsc[:, 1, :], nsc[:, 1, :], 1e-12, None, ALU.max))
            link3(d.reciprocal(nsc[:, 2, :], nsc[:, 1, :]))
            link3(d.tensor_tensor(comb, comb, by_node(nsc[:, 2, :]), ALU.mult))
            link3(d.tensor_tensor(comb, comb, x2, ALU.add))
            assert cnt[0] == ND_LN2
            norm(link3, s.nd_a, 5, comb, gb, nsc, x2)
            link3(d.tensor_tensor(xs[1], x2, by_node(dout), ALU.mult))
            link3(d.tensor_scalar(gb.rearrange("p a f -> p (a f)"), xs[1].rearrange("p a f -> p (a f)"), ALPHA, None, ALU.mult))
            assert cnt[0] == ND_L3
            with v.Fori(0, (K3 - 2) // 2) as kk:
                for par in range(2):
                    post_chunks(2 * kk + (K2 + par), xs[(1 + par) % 2], xs[par % 2], step3(a_mid))
            post_chunks(KTOT - 2, xs[1], xs[0], step3(a_mid))
            v.wait_ge(s.xs_v, NPOS * (KTOT - 1))
            link3(d.tensor_scalar(gb.rearrange("p a f -> p (a f)"), x2.rearrange("p a f -> p (a f)"), ALPHA, None, ALU.mult))
            post_chunks(KTOT - 1, xs[0], xs[1], step3(a_last))
            v.wait_ge(s.xs_v, NPOS * KTOT)
            link3(d.tensor_tensor(comb, xs[1], x2, ALU.add))
            assert cnt[0] == ND_LN3, cnt[0]
            norm(link3, s.nd_a, 7, comb, gb, nsc, xs[0])
            assert cnt[0] == ND_OUT, cnt[0]

        @block.scalar
        def _(act):
            a = nc.scalar
            start_rings(act, [s.pair_e])
            for q in range(2):
                act.dma_start(first2[0:1, q:q + 1], lw[0:1].rearrange("(o k) -> o k", o=1)).then_inc(s.stg[q], 16)
            act.dma_start(xa, x.rearrange("(a p) f -> p a f", p=P)).then_inc(s.ld_x, 16)
            act.dma_start(beB, be.rearrange("(o f) -> o f", o=1).to_broadcast([P, F])).then_inc(s.ld_wts, 16)
            act.wait_ge(s.consts, C_FIRST)
            act.dma_start(w1ab[0:F, 0:F], W1_0[0:F, :]).then_inc(s.ld_wts, 16)
            act.dma_start(w1ab[0:F, F:P], W1_0[F:2 * F, :]).then_inc(s.ld_wts, 16)
            act.dma_start(w2p[0:F, 0:F], W2_0).then_inc(s.ld_wts, 16)
            act.dma_start(w2p[F:F + 1, 0:F], b2_0.rearrange("(o f) -> o f", o=1)).then_inc(s.ld_wts, 16)
            act.dma_start(w1ab[F:F + 1, F:P], b1_0.rearrange("(o f) -> o f", o=1)).then_inc(s.ld_wts, 16)
            for b in range(2):
                for half in range(2):
                    row = (SPAN + 1) * half + SPAN
                    act.dma_start(QD[row:row + 1, b, F * half:F * half + F], W1_0[2 * F:2 * F + 1, :]).then_inc(s.ld_wts, 16)
            for g4 in range(7):
                w_ = min(CH, NP - CH * g4)
                act.wait_ge(s.xt_t, g4 + 1)
                a.activation(xT[0:F, CH * g4:CH * g4 + w_], banks[6 + g4 % 2][0:F, 0:w_], ACT.Copy).then_inc(s.xt_c, 1)
            for g4 in range(7):
                n = min(4, NB - 4 * g4)
                act.wait_ge(s.pq_t, g4 + 1)
                a.activation(PQ[:, 4 * g4:4 * g4 + n, :].rearrange("p a f -> p (a f)"), banks[2 + g4 % 2][:, 0:P * n], ACT.Copy).then_inc(s.pq_c, 1)
            recv = rec.rearrange("p (i j) f -> p i j f", j=8)
            for j in range(8):
                act.wait_ge(s.rec_t, j + 1)
                a.activation(recv[:, :, j, :], banks[j % 2][:, 0:4 * NSB].rearrange("p (f i) -> p i f", f=4), ACT.Copy).then_inc(s.rec_c, 1)

            def product_copy(r, h, b):
                act.wait_ge(r.tr[b], h + 1 + 1)
                act.wait_ge(r.pre[b], h + 1)
                if r is R[0]:
                    a.activation(OHT[:, b, :], psT[0:2 * (SPAN + 1), :], ACT.Copy).then_inc(r.trc[b], 1)
                else:
                    a.activation(EAT[:, b, :], psT[:, 0:2 * P], ACT.Copy).then_inc(r.trc[b], 1)

            def superblock(r, i, h, b, k, kh, q, mb, qh, more):
                act.wait_ge(r.add[b], h + 1 + 1)
                gflat = G[:, b].rearrange("p k f -> p (k f)")
                a.activation(gflat, gflat, ACT.Relu).then_inc(r.relu[b], 1)
                hn, bn = following(h, b)
                if more:
                    product_copy(r, hn, bn)
                if k is not None:
                    act.wait_ge(s.pair_t[b], kh + 1 + 1)
                    prod = psW[b].rearrange("p (c j) -> p c j", j=PAIR)
                    if q is not None:
                        act.wait_ge(s.stg[q], 16 * qh + 16)
                        a.activation(Wres[:, :, ds(PAIR * k, PAIR)], prod[:, 0:RES, :], ACT.Copy).then_inc(s.pair_e[b], 1)
                        a.activation(stage[:, q, :, ds(PAIR * mb, PAIR)], prod[:, RES:NB, :], ACT.Copy).then_inc(s.pair_e[b], 1)
                    else:
                        a.activation(Wres[:, :, PAIR * k:PAIR * k + PAIR], prod[:, 0:RES, :], ACT.Copy).then_inc(s.pair_e[b], 1)
                        a.activation(W6[:, :, PAIR * mb:PAIR * mb + PAIR], prod[:, RES:NB, :], ACT.Copy).then_inc(s.pair_e[b], 1)

            def quarter_end(Q, q, qh):
                if q is None:
                    return
                act.wait_ge(s.pair_e[0], 8 * Q + 8 + 1)
                act.wait_ge(s.pair_e[1], 8 * Q + 8 + 1)
                act.dma_start(d_w[:, ds(Q, 1), :, :].rearrange("p o a e -> p o (a e)"),
                              stage[:, q:q + 1, :, :].rearrange("p o a e -> p o (a e)")).then_inc(s.stg[q], 16)

            def norm(v_sem, v_at, y, tmp_, sc, a_sem):
                act.wait_ge(v_sem, v_at)
                a.activation(tmp_, y, ACT.Square).then_inc(a_sem, 1)
                act.wait_ge(v_sem, v_at + 2)
                a.activation(sc[:, 4, :], sc[:, 3, :], ACT.Sqrt).then_inc(a_sem, 1)

            product_copy(R[0], 0, 0)
            edge_loop(act, 0, superblock, quarter_end)
            norm(s.nb_v, NB_Y + 3, lnA, lnB, lnS, s.nb_a)
            act.wait_ge(s.nb_v, NB_X1 + 1)
            act.dma_start(d_t1.rearrange("(a p) f -> p a f", p=P), lnB).then_inc(s.st_t1, 16)
            product_copy(R[1], 0, 0)
            edge_loop(act, 1, superblock, quarter_end)
            act.wait_ge(s.ld_l1, 7 * 16)
            act.wait_ge(s.nc_v, 4)
            for g4 in range(7):
                w_ = min(CH, NP - CH * g4)
                act.wait_ge(s.nc_t, NCT_X1 + g4 + 1)
                a.activation(h1T[0:F, CH * g4:CH * g4 + w_], banks[(4 + g4) % 7][0:F, 0:w_], ACT.Relu, bias=b1n).then_inc(s.nc_a, 1)
            for g5 in range(5):
                act.wait_ge(s.nc_t, NCT_H1 + g5 + 1)
                a.activation(lnA[:, 5 * g5:5 * g5 + 5, :], banks[H2B[g5]][:, 0:5 * HALF].rearrange("p (a c) -> p a c", c=HALF)[:, :, 0:F],
                             ACT.Copy).then_inc(s.nc_a, 1)
            act.wait_ge(s.nc_v, NC_DEG)
            act.dma_start(lwt[:, 0:4], lw.rearrange("(o k) -> o k", o=1).to_broadcast([P, 4])).then_inc(s.ld_lw, 16)
            a.activation(nsc[:, 7:9, :], nsc[:, 4:6, :], ACT.Sqrt).then_inc(s.nc_a, 1)
            norm(s.nc_v, NC_LEAKY + 3, lnA, lnB, lnS, s.nc_a)
            norm(s.nc_v, NC_LEAKY + 13, lnA, lnB, lnS, s.nc_a)
            act.wait_ge(s.nd_v, 3)
            a.activation(lwt[:, 6:10], lwt[:, 0:4], ACT.Exp, bias=lwt[:, 5:6]).then_inc(s.nd_a, 1)

            def product(k):
                for t_, c in enumerate(CORDER):
                    act.wait_ge(s.acc_t, NPOS * k + t_ + 1)
                    if t_ >= 3:
                        act.wait_ge(s.out_t, NPOS * k + t_ - 2)
                    if c < NCH:
                        a.activation(accS[:, t_ % 3, :], banks[t_ % 4][:, :], ACT.Copy).then_inc(s.acc_c, 1)
                    else:
                        a.activation(accL[:, 0:LASTW], banks[t_ % 4][:, 0:LASTW], ACT.Copy).then_inc(s.acc_c, 1)
            for k in range(K2):
                product(k)
            act.wait_ge(s.xs_v, NPOS * K2)
            a.activation(gb, comb, ACT.Square).then_inc(s.nd_a, 1)
            act.wait_ge(s.nd_v, ND_DOUT)
            a.activation(nsc[:, 9, :], nsc[:, 6, :], ACT.Sqrt).then_inc(s.nd_a, 1)
            act.wait_ge(s.nd_v, ND_DOUT + 4)
            a.activation(nsc[:, 1, :], nsc[:, 0, :], ACT.Sqrt).then_inc(s.nd_a, 1)
            norm(s.nd_v, ND_LN2 + 3, comb, gb, nsc, s.nd_a)
            with act.Fori(0, (K3 - 2) // 2) as kk:
                for par in range(2):
                    product(2 * kk + (K2 + par))
            product(KTOT - 2)
            product(KTOT - 1)
            norm(s.nd_v, ND_LN3 + 3, comb, gb, nsc, s.nd_a)

        @block.tensor
        def _(pe):
            t = nc.tensor
            start_rings(pe, [s.pair_t] + [x for r in R for x in (r.pre, r.tr, r.seg)])
            pe.wait_ge(s.consts, C_ALL)
            pe.wait_ge(s.ld_x, 16)
            for g4 in range(7):
                if g4 >= 2:
                    pe.wait_ge(s.xt_c, g4 - 1)
                for n in range(4 * g4, min(4 * g4 + 4, NB)):
                    last = t.transpose(banks[6 + g4 % 2][0:F, P * (n % 4):P * (n % 4) + P], xa[:, n, :], ident)
                last.then_inc(s.xt_t, 1)
            pe.wait_ge(s.ld_wts, WTS)
            for g4 in range(7):
                pe.wait_ge(s.xt_c, g4 + 1)
                if g4 >= 2:
                    pe.wait_ge(s.pq_c, g4 - 1)
                for n in range(4 * g4, min(4 * g4 + 4, NB)):
                    last = t.matmul(banks[2 + g4 % 2][:, P * (n % 4):P * (n % 4) + P], xT[0:F + 1, P * n:P * n + P],
                                    w1ab[0:F + 1, :], start=True, stop=True)
                last.then_inc(s.pq_t, 1)
            pe.wait_ge(s.prep_v, V_FLD)
            for j in range(8):
                if j >= 2:
                    pe.wait_ge(s.rec_c, j - 1)
                for f in range(4):
                    last = t.transpose(banks[j % 2][:, NSB * f:NSB * f + NSB], fld[f][:, P * j:P * j + P], ident[0:NSB, 0:NSB])
                last.then_inc(s.rec_t, 1)

            def transposes(r, h, b):
                hp, bp = (h, 1) if b == 0 else (h + 1, 0)
                if r is R[0]:
                    pe.wait_ge(r.oh[b], 2 * h + 2)
                    for j in range(4):
                        last = t.transpose(psT[0:2 * (SPAN + 1), P * j:P * j + P],
                                           OH[:, b, 2 * j:2 * j + 2, :].rearrange("p k c -> p (k c)"), ident)
                else:
                    pe.wait_ge(r.ea[b], 16 * (h + 1))
                    for j in range(2):
                        last = t.transpose(psT[:, P * j:P * j + P], EA[:, b, P * j:P * j + P], ident)
                last.then_inc(r.tr[b], 1)

            def products(r, h, b):
                pe.wait_ge(r.trc[b], h + 1)
                pe.wait_ge(r.add[b], h + 1)
                if r is R[0]:
                    pe.wait_ge(r.qd[b], 32 * (h + 1))
                    for j in range(4):
                        last = t.matmul(psPre[b][:, P * j:P * j + P], OHT[:, b, P * j:P * j + P], QD[:, b, :], start=True, stop=True)
                else:
                    for j in range(2):
                        last = t.matmul(psPre[b][:, 2 * P * j:2 * P * j + 2 * P], EAT[:, b, P * j:P * j + P], WEBD, start=True, stop=True)
                last.then_inc(r.pre[b], 1)

            def superblock(r, i, h, b, k, kh, q, mb, qh, more):
                pe.wait_ge(r.relu[b], h + 1)
                pe.wait_ge(r.oh[b], 2 * h + 2)
                pe.wait_ge(r.agg[b], h + 1)
                for j in range(8):
                    beside = ones if r is R[0] else OH[:, b, j, SPAN:SPAN + 1]
                    t.matmul(psSeg[0:F, P * b:P * b + SPAN], G[:, b, j, :], OH[:, b, j, 0:SPAN], start=j == 0, stop=j == 7)
                    last = t.matmul(psSeg[F:P, P * b:P * b + SPAN], beside.to_broadcast([P, F]), OH[:, b, j, 0:SPAN],
                                    start=j == 0, stop=j == 7)
                last.then_inc(r.seg[b], 1)
                hn, bn = following(h, b)
                if more:
                    pe.wait_ge(r.trc[b], h + 1)
                    transposes(r, hn, bn)
                    products(r, hn, bn)
                if k is not None:
                    pe.wait_ge(s.pair_v[b], kh + 1 + 1)
                    pe.wait_ge(s.pair_e[b], 2 * kh + 1)
                    prod = psW[b].rearrange("p (c j) -> p c j", j=PAIR)
                    for w in range(2):
                        for j in range(TPW):
                            last = t.matmul(prod[:, :, WIN * w:WIN * w + WIN], alo[:, b, TPW * w + j, :],
                                            outer[:, b, TPW * w + j, :].rearrange("p (c j) -> p c j", j=WIN), start=j == 0, stop=j == TPW - 1)
                    last.then_inc(s.pair_t[b], 1)

            transposes(R[0], 0, 0)
            products(R[0], 0, 0)
            edge_loop(pe, 0, superblock)
            pe.wait_ge(R[0].agg[0], NSB // 2 + 1 + 1)
            pe.wait_ge(R[0].agg[1], NSB // 2 + 1)
            pe.wait_ge(s.pair_e[0], NLOOP + 1)
            pe.wait_ge(s.pair_e[1], NLOOP + 1)
            for g5 in range(5):
                for n in range(5):
                    lo_ = P * (5 * g5 + n)
                    last = t.matmul(banks[g5][:, HALF * n:HALF * n + HALF], aggT[0:F + 1, lo_:lo_ + P], w2p[0:F + 1, :], start=True, stop=True)
                last.then_inc(s.nb_t, 1)
            pe.wait_ge(s.nb_v, NB_Y)
            transposes(R[1], 0, 0)
            pe.wait_ge(s.ld_we, 4 * 16)
            products(R[1], 0, 0)
            edge_loop(pe, 1, superblock)
            pe.wait_ge(R[1].agg[0], NSB // 2 + 1 + 1)
            pe.wait_ge(R[1].agg[1], NSB // 2 + 1)
            pe.wait_ge(s.pair_e[0], NPAIR + 1)
            pe.wait_ge(s.pair_e[1], NPAIR + 1)
            for g4 in range(7):
                for n in range(4 * g4, min(4 * g4 + 4, NB)):
                    last = t.transpose(banks[g4][0:F, P * (n % 4):P * (n % 4) + P], xa[:, n, :], ident)
                last.then_inc(s.nc_t, 1)
            pe.wait_ge(s.nc_v, NC_HT)
            for g4 in range(7):
                w_ = min(CH, NP - CH * g4)
                t.matmul(banks[(4 + g4) % 7][0:F, 0:w_], w1n, hT[0:F, CH * g4:CH * g4 + w_], start=True, stop=True).then_inc(s.nc_t, 1)
            pe.wait_ge(s.nc_a, NCA_H1)
            for g5 in range(5):
                for n in range(5):
                    lo_ = P * (5 * g5 + n)
                    last = t.matmul(banks[H2B[g5]][:, HALF * n:HALF * n + HALF], h1T[0:F + 1, lo_:lo_ + P], w2n, start=True, stop=True)
                last.then_inc(s.nc_t, 1)
            pe.wait_ge(s.nc_a, NCA_H1 + 2)
            for g5 in range(5):
                for n in range(5):
                    lo_ = P * (5 * g5 + n)
                    last = t.matmul(banks[DEGB[g5]][:, HALF * n:HALF * n + HALF], aggT[:, lo_:lo_ + P], sel, start=True, stop=True)
                last.then_inc(s.nc_t, 1)

            def fold_chunk(k, t_, c):
                pe.wait_ge(s.acc_c, NPOS * k + t_ + 1)
                if t_ >= 4:
                    pe.wait_ge(s.xs_v, NPOS * k + t_ - 3)
                for n in range(4 if c < NCH else 1):
                    left = accS[:, t_ % 3, P * n:P * n + P] if c < NCH else accL
                    last = t.matmul(banks[4 + t_ % 4][:, HALF * n:HALF * n + HALF], left, fold, start=True, stop=True)
                last.then_inc(s.out_t, 1)

            def product(k, old, first=False):
                if not first:
                    pe.wait_ge(s.xs_v, NPOS * k - 1)
                for t_, c in enumerate(CORDER):
                    w_ = CH if c < NCH else LASTW
                    if t_ >= 4:
                        pe.wait_ge(s.acc_c, NPOS * k + t_ - 3)
                    for n in range(NB):
                        piece = NPC * c + (n - RES) // PIECE
                        if n == 20 and t_ == 0 and not first:
                            pe.wait_ge(s.xs_v, NPOS * k)
                        if n < RES:
                            right = Wres[:, n, CH * c:CH * c + w_]
                        elif c == NCH:
                            right = W6[:, n - RES, :]
                        else:
                            if (n - RES) % PIECE == 0:
                                pe.wait_ge(s.pc[piece % RING], 16 * (NPIECE // RING * k + piece // RING + 1))
                            right = ring[:, piece % RING, :].rearrange("p (q a e) -> p a q e", q=CH // QC, e=QC)[:, (n - RES) % PIECE, :, :]
                        last = t.matmul(banks[t_ % 4][F * (n % 2):F * (n % 2) + F, 0:w_], old[:, n, :], right, start=n < 2, stop=n >= NB - 2)
                        if c < NCH and n < NB - 1 and n >= RES and (n - RES) % PIECE == PIECE - 1:
                            last.then_inc(s.pc_free, 1)
                        if n == RES - 1 and t_ >= 1:
                            fold_chunk(k, t_ - 1, CORDER[t_ - 1])
                    last.then_inc(s.acc_t, 1)
                fold_chunk(k, NPOS - 1, CORDER[-1])

            pe.wait_ge(s.nd_v, 1)
            for k in range(K2):
                product(k, xs[k % 2], k == 0)
            pe.wait_ge(s.nd_v, ND_L3)
            with pe.Fori(0, (K3 - 2) // 2) as kk:
                for par in range(2):
                    product(2 * kk + (K2 + par), xs[(1 + par) % 2])
            product(KTOT - 2, xs[1])
            product(KTOT - 1, xs[0])


_INS = ["x", "src", "dst", "edge_attr_32", "edge_weight", "edge_weight1", "L0_gnn_W1", "L0_gnn_b1",
        "L0_gnn_W2", "L0_gnn_b2", "L1_gnn_We", "L1_gnn_be", "L1_gnn_W1", "L1_gnn_b1", "L1_gnn_W2",
        "L1_gnn_b2", "L1_gnn_eps_gin", "L1_gnn_gamma", "L1_gnn_beta", "L2_gnn_layer_weights"]


def kernel(**inputs):
    import concourse.bacc as _bacc
    from concourse.bass_utils import run_bass_kernel_spmd as _run

    pads = {"x": (NP, 0), "src": (EP, 0), "dst": (EP, NP), "edge_attr_32": (EP, 0),
            "edge_weight": (EP, 0), "edge_weight1": (EP, 0)}
    nc = _bacc.Bacc("TRN2", target_bir_lowering=False, num_devices=1)
    arrays, args = {}, []
    for name in _INS:
        a = np.ascontiguousarray(inputs[name])
        if name == "edge_weight1":
            a = a.reshape(E)
        if name == "L1_gnn_eps_gin":
            a = a.reshape(1)
        if name in pads:
            rows, fill = pads[name]
            full = np.full((rows,) + a.shape[1:], fill, a.dtype)
            full[:a.shape[0]] = a
            a = full
        arrays[f"in_{name}"] = a
        args.append(nc.dram_tensor(f"in_{name}", a.shape, mybir.dt.from_np(a.dtype), kind="ExternalInput").ap())
    args.append(nc.dram_tensor("out_0", (N, F), mybir.dt.float32, kind="ExternalOutput").ap())
    build(nc, *args)
    return _run(nc, [arrays], core_ids=[0]).results[0]["out_0"]
```

```python
from contextlib import ExitStack

import numpy as np

import concourse.bass as bass
from concourse import mybir

N, F, E, ED = 3125, 64, 103125, 32
P = 128
NB = -(-N // P)
NP = NB * P
SBE = 8 * P
NSB = -(-E // SBE)
EP = NSB * SBE
NT = EP // P
WIN = 8
PAIR = 2 * WIN
CH = 512
NCH = N // CH
LASTW = 64
NCOL = NCH * CH + LASTW
NPAIR = NCOL // PAIR
NWIN = 2 * NPAIR
TPW = 4
RES = 9
STR = NB - RES
QC = 128
SPAN = 47
PIECE = 4
NPC = STR // PIECE
RING = 6
TURN_AT = 5
WTS = 16 * 10
HALF = 96
EPS = 1e-5
ALPHA = 0.1
K2, K3 = 3, 10
KTOT = K2 + K3
CORDER = [0, NCH] + list(range(1, NCH))
NPOS = NCH + 1
NPIECE = NCH * NPC
TINY = float(np.finfo(np.float32).tiny)

C_FIRST, C_ALL = 12, 13
V_FLD, V_ROWS = 9, 34
NB_Y, NB_X1, NB_WEBD = 5, 12, 15
NC_HT, NC_DEG, NC_LEAKY, NC_X2 = 11, 19, 24, 41
NCT_X1, NCT_H1, NCT_H2, NCT_DEG = 7, 14, 19, 24
NCA_H1, NCA_H2, NCA_ROOT = 7, 12, 13
DEGB = (4, 5, 6, 7, 0)
H2B = (7, 0, 1, 2, 3)
ND_L2, ND_DOUT, ND_LN2, ND_L3, ND_LN3, ND_OUT = 7, 10, 18, 27, 29, 36


class Signals:
    pass


def build(nc, x, src, dst, eattr, ew, ew1, W1_0, b1_0, W2_0, b2_0, We, be, W1_1, b1_1, W2_1, b2_1,
          eps_gin, gamma, beta, lw, out):
    f32, i32 = mybir.dt.float32, mybir.dt.int32
    ALU, ACT, AX = mybir.AluOpType, mybir.ActivationFunctionType, mybir.AxisListType.X
    ds = bass.ds
    ctx = ExitStack()
    with ctx:
        def sem(name):
            return ctx.enter_context(nc.semaphore(name))

        WORDS = 53200
        arena = ctx.enter_context(nc.sbuf_tensor("arena", [P, WORDS], f32))
        top = [0]

        def take(words):
            at = top[0]
            top[0] += words
            assert top[0] <= WORDS, (top[0], WORDS)
            return at

        def at(start, *shape, parts=P, part0=0):
            n = int(np.prod(shape))
            ap = arena[part0:part0 + parts, start:start + n]
            if len(shape) == 2:
                ap = ap.rearrange("p (a b) -> p a b", b=shape[1])
            if len(shape) == 3:
                ap = ap.rearrange("p (a b c) -> p a b c", b=shape[1], c=shape[2])
            return ap

        o_wres = take(RES * NCOL)
        o_w6 = take(STR * LASTW)
        o_iota = take(P)
        o_ident = take(P)
        o_w1ab = take(P)
        o_w2 = take(HALF)
        o_be = take(F)
        o_hi1 = take(2 * TPW * NB)
        o_small = take(111)
        o_lo = top[0]
        Wres = at(o_wres, RES, NCOL)
        W6 = at(o_w6, STR, LASTW)
        iota = at(o_iota, P)
        ident = at(o_ident, P)
        w1ab = at(o_w1ab, P)
        w2p = at(o_w2, HALF)
        beB = at(o_be, F)
        hi1 = at(o_hi1, 2 * TPW, NB)
        ones = at(o_small, 1)
        edge8 = at(o_small + 1, 8, parts=NWIN // 4)
        wcols = at(o_small + 9, PAIR)
        wcols0 = at(o_small + 25, PAIR)
        first2 = at(o_small + 105, 2)
        dsel = at(o_small + 41, 2 * TPW, WIN)
        flag = at(o_small + 107, 1, parts=1).bitcast(i32)
        worst = at(o_small + 108, 3, parts=1)

        o_xa = take(NB * F)
        o_agg = take(NP)
        o_stage = take(2 * STR * QC)
        o_alo = take(2 * 2 * TPW * P)
        o_outer = take(2 * 2 * TPW * NB * WIN)
        o_rec = take(NT * 4)
        o_g = take(2 * 8 * F)
        o_oh = take(2 * 8 * (SPAN + 1))
        o_oht = take(2 * 4 * P)
        o_qd = take(2 * P)
        o_rel = take(NSB * 8)
        o_ew = take(NSB * 8)
        o_wrec = take(2 * 2 * TPW * 4)
        o_base = take(NSB)
        o_idx = take(2 * 8)
        o_lorow = take(NWIN)
        xa = at(o_xa, NB, F)
        aggT = at(o_agg, NP)
        stage = at(o_stage, 2, STR, QC)
        alo = at(o_alo, 2, 2 * TPW, P)
        outer = at(o_outer, 2, 2 * TPW, NB * WIN)
        rec = at(o_rec, NT, 4)
        G = at(o_g, 2, 8, F)
        OH = at(o_oh, 2, 8, SPAN + 1)
        OHT = at(o_oht, 2, 4 * P, parts=2 * (SPAN + 1))
        QD = at(o_qd, 2, P, parts=2 * (SPAN + 1))
        EA = at(o_oht + 512, 2, 256)
        EAT = at(o_oht, 2, 256)
        WEBD = at(o_qd, 256)
        rel = at(o_rel, NSB * 8)
        ewall = at(o_ew, NSB, 8)
        ewflat = at(o_ew, NSB * 8)
        wrec = at(o_wrec, 2, 2 * TPW, 4)
        base_row = at(o_base, NSB, parts=1).bitcast(i32)
        idx = at(o_idx, 2, 8).bitcast(i32)
        lo_row = at(o_lorow, NWIN, parts=1).bitcast(i32)

        t = [o_wres]

        def tmp(words):
            a = t[0]
            t[0] += words
            assert t[0] <= o_iota
            return a
        dstN = at(tmp(SBE), SBE, parts=NSB).bitcast(i32)
        srcN = at(tmp(SBE), SBE, parts=NSB).bitcast(i32)
        fld = [at(tmp(SBE), SBE, parts=NSB) for _ in range(4)]
        srcI = [at(tmp(SBE), SBE, parts=NSB).bitcast(i32) for _ in range(2)]
        o_tm = tmp(NSB * 17)
        tmin = at(o_tm, NSB * 0 + 8, parts=NSB)
        tmax = at(o_tm + 8, 8, parts=NSB)
        bmin = at(o_tm + 16, 1, parts=NSB)
        tminB = at(tmp(NT), NT)
        tmaxB = at(tmp(NT), NT)
        bB = at(tmp(NSB), NSB)
        bad = at(tmp(3 * NT), 3, NT, parts=1)
        WQ = NWIN // 4
        c1 = at(tmp(NT), NT, parts=WQ)
        c2 = at(tmp(NT), NT, parts=WQ)
        tiota = at(tmp(NT), NT)
        lohi = at(tmp(32), 32, parts=WQ)
        lo_i = lohi[:, 8:12].bitcast(i32)
        dstS = at(tmp(NSB * 8), NSB, 8).bitcast(i32)
        PQ = at(tmp(NB * P), NB, P)
        xT = at(tmp(NP), NP)

        iotaW = at(o_stage, NP)
        genB = [at(o_alo, NCOL), at(o_g, NCOL)]
        genA = [at(o_g + NCOL + P * b, P) for b in range(2)]
        assert NCOL <= o_rec - o_alo and NCOL + 2 * P <= o_ew - o_g
        gen_row = at(o_agg, NCH * CH)
        gen_cur = [at(o_wrec + 4 * b, 4) for b in range(2)]
        gen_wn = [at(o_wrec + 8 + b, 1) for b in range(2)]
        gen_n = at(o_wrec + 10, 1)
        dcol = at(o_wrec, 8)
        wcol = at(o_wrec + 8, 8)
        genOH = [at(o_alo + CH * b, CH) for b in range(2)]
        w1c = at(o_oh, F)

        lnA = at(o_outer, NB, F)
        lnB = at(o_alo, NB, F)
        lnS = at(o_outer + NB * F, 8, NB)
        hT = at(o_stage, NP)
        h1T = at(o_rec, NP)
        o_l1 = o_g
        w1n = at(o_l1, F, parts=F)
        w2n = at(o_l1 + F, HALF, parts=F + 1)
        b1n = at(o_l1 + F + HALF, 1, parts=F)
        epsn = at(o_l1 + F + HALF + 1, 1)
        gam = at(o_l1 + F + HALF + 2, F)
        bet = at(o_l1 + 2 * F + HALF + 2, F)
        sel = at(o_l1 + 3 * F + HALF + 2, HALF)

        top[0] = o_lo
        x2 = at(take(NB * F), NB, F)
        assert o_lo == o_xa
        o_ring = take(RING * PIECE * CH)
        ring = at(o_ring, RING, PIECE * CH)
        xs = [at(take(NB * F), NB, F) for _ in range(2)]
        comb = at(take(NB * F), NB, F)
        gb = at(take(NB * F), NB, F)
        accS = at(take(3 * CH), 3, CH)
        accL = at(take(P), P)
        post = at(take(4 * F), 4, F)
        nsc = at(take(12 * NB), 12, NB)
        lwt = at(take(16), 16)
        deg_str = at(take((NCH + 1) * STR), NCH + 1, STR)

        banks = [ctx.enter_context(nc.psum_tensor(f"bank{i}", [P, CH], f32)) for i in range(8)]
        psW = [banks[0][:, 0:NB * PAIR], banks[1][:, 0:NB * PAIR]]
        psPre = [banks[2], banks[3]]
        psT = banks[4]
        psSeg = banks[5]

        def dram(name, shape, dt=f32):
            return nc.dram_tensor(name, shape, dt, kind="Internal").ap()
        d_p = dram("d_p", [NP, F])
        d_q = dram("d_q", [NP, F])
        d_t1 = dram("d_t1", [NP, F])
        d_tmin = dram("d_tmin", [NT])
        d_tmax = dram("d_tmax", [NT])
        d_bmin = dram("d_bmin", [NSB])
        d_lo = dram("d_lo", [1, NWIN], i32)
        d_w = dram("d_w", [P, NCH * CH // QC, STR, QC])

        def two(name):
            return [sem(name + "_0"), sem(name + "_1")]
        s = Signals()
        s.consts = sem("consts")
        s.ld_edges = sem("ld_edges")
        s.ld_sb = sem("ld_sb")
        s.ld_x = sem("ld_x")
        s.ld_wts = sem("ld_wts")
        s.ld_bc = sem("ld_bc")
        s.st_min = sem("st_min")
        s.st_rows = sem("st_rows")
        s.st_p = sem("st_p")
        s.st_q = sem("st_q")
        s.prep_v = sem("prep_v")
        s.rec_t = sem("rec_t")
        s.rec_c = sem("rec_c")
        s.xt_t = sem("xt_t")
        s.xt_c = sem("xt_c")
        s.pq_t = sem("pq_t")
        s.pq_c = sem("pq_c")
        s.wrec = two("wrec")
        s.pair_step = sem("pair_step")
        s.pair_v = two("pair_v")
        s.pair_t = two("pair_t")
        s.pair_e = two("pair_e")
        s.deg_v = sem("deg_v")
        s.stg = two("stg")
        s.nb_v = sem("nb_v")
        s.nb_a = sem("nb_a")
        s.nb_t = sem("nb_t")
        s.st_t1 = sem("st_t1")
        s.ld_w = sem("ld_w")
        s.ld_we = sem("ld_we")
        s.nc_v = sem("nc_v")
        s.nc_a = sem("nc_a")
        s.nc_t = sem("nc_t")
        s.ld_l1 = sem("ld_l1")
        s.ld_lw = sem("ld_lw")
        s.pc = [sem(f"pc{i}") for i in range(RING)]
        s.pc_free = sem("pc_free")
        s.acc_t = sem("acc_t")
        s.acc_c = sem("acc_c")
        s.out_t = sem("out_t")
        s.post_v = sem("post_v")
        s.xs_v = sem("xs_v")
        s.comb_v = sem("comb_v")
        s.nd_v = sem("nd_v")
        s.nd_a = sem("nd_a")
        s.st_out = sem("st_out")

        s.bad = sem("bad")
        s.flag = sem("flag")
        s.gen_iota = sem("gen_iota")
        s.gen_step = sem("gen_step")
        s.gen_op = two("gen_op")
        s.gen_mm = two("gen_mm")
        s.gen_out = sem("gen_out")
        s.gen_st = sem("gen_st")
        s.gen_clear = sem("gen_clear")
        s.gen_w1c = sem("gen_w1c")

        def layer_signals(layer):
            r = Signals()
            r.idx = two(f"idx{layer}")
            r.qd = two(f"qd{layer}")
            r.g = two(f"g{layer}")
            r.oh = two(f"oh{layer}")
            r.tr = two(f"tr{layer}")
            r.trc = two(f"trc{layer}")
            r.pre = two(f"pre{layer}")
            r.add = two(f"add{layer}")
            r.relu = two(f"relu{layer}")
            r.seg = two(f"seg{layer}")
            r.agg = two(f"agg{layer}")
            r.ea = two(f"ea{layer}")
            r.m_ld = sem(f"m_ld{layer}")
            r.m_dst = sem(f"m_dst{layer}")
            r.m_g = sem(f"m_g{layer}")
            r.m_step = sem(f"m_step{layer}")
            r.m_tr = sem(f"m_tr{layer}")
            r.m_trc = sem(f"m_trc{layer}")
            r.m_pre = sem(f"m_pre{layer}")
            r.m_msg = sem(f"m_msg{layer}")
            r.m_oh = two(f"m_oh{layer}")
            r.m_mm = two(f"m_mm{layer}")
            r.m_agg = sem(f"m_agg{layer}")
            return r
        R = [layer_signals(0), layer_signals(1)]

        block = ctx.enter_context(nc.Block())

        NLOOP = NCH // 2 * CH // PAIR
        NQ = NCH * CH // QC

        def edge_loop(eng, layer, superblock, quarter_end=None):
            r = R[layer]
            with eng.Fori(0, NLOOP // 16) as u:
                for q in range(2):
                    with eng.Fori(0, 4) as m:
                        for b in range(2):
                            h = 8 * u + 4 * q + m
                            kh = h + layer * (NLOOP // 2)
                            superblock(r, 2 * h + b, h, b, 2 * kh + b, kh, q, 2 * m + b, u + layer * (NLOOP // 16), True)
                    if quarter_end:
                        quarter_end(2 * u + q + layer * (NLOOP // 8), q, u + layer * (NLOOP // 16))
            for i in range(NLOOP, NSB):
                k = i + NLOOP
                if layer == 0 or k >= NPAIR:
                    k = None
                superblock(r, i, i // 2, i % 2, k, None if k is None else k // 2, None, i - NLOOP, None, i + 1 < NSB)
            if layer == 1 and quarter_end:
                quarter_end(NQ, None, None)

        def by_order(eng, general, ordered):
            is_bad = eng.value_load(flag, min_val=0, max_val=1)
            with eng.If(is_bad > 0):
                general()
            with eng.Else():
                ordered()

        def blocks(eng, block_):
            with eng.Fori(0, RES) as n:
                block_(n, True)
            with eng.Fori(RES, NB) as n:
                block_(n, False)

        def chunks(eng, chunk):
            with eng.Fori(0, NCH) as c:
                chunk(c, CH)
            chunk(NCH, NP - NCH * CH)

        def following(h, b):
            return (h, 1) if b == 0 else (h + 1, 0)

        def rows(t, i):
            return t.rearrange("(i p k) -> i p k", p=P, k=8)[ds(i, 1), :, :].rearrange("o p k -> p (o k)")

        def start_rings(eng, names):
            for x in names:
                for each in x:
                    eng.sem_inc(each, 1)

        @block.sync
        def _(sp):
            sp.dma_start(dstN, dst.rearrange("(p e) -> p e", e=SBE)).then_inc(s.ld_edges, 16)
            sp.dma_start(srcN, src.rearrange("(p e) -> p e", e=SBE)).then_inc(s.ld_edges, 16)
            sp.dma_start(fld[3], ew.rearrange("(p e) -> p e", e=SBE)).then_inc(s.ld_edges, 16)
            sp.wait_ge(s.prep_v, 5)
            sp.dma_start(d_tmin.rearrange("(p k) -> p k", k=8), tmin).then_inc(s.st_min, 16)
            sp.dma_start(d_tmax.rearrange("(p k) -> p k", k=8), tmax).then_inc(s.st_min, 16)
            sp.dma_start(d_bmin.rearrange("(p k) -> p k", k=1), bmin).then_inc(s.st_min, 16)
            sp.wait_ge(s.st_min, 48)
            sp.dma_start(bB, d_bmin.rearrange("(o k) -> o k", o=1).to_broadcast([P, NSB])).then_inc(s.ld_bc, 16)
            sp.dma_start(tminB, d_tmin.rearrange("(o k) -> o k", o=1).to_broadcast([P, NT])).then_inc(s.ld_bc, 16)
            sp.dma_start(tmaxB, d_tmax.rearrange("(o k) -> o k", o=1).to_broadcast([P, NT])).then_inc(s.ld_bc, 16)
            sp.dma_start(dstS, dst.rearrange("(i p k) -> p i k", p=P, k=8)).then_inc(s.ld_sb, 16)
            sp.dma_start(ewall, ew1.rearrange("(i p k) -> p i k", p=P, k=8)).then_inc(s.ld_sb, 16)
            for done, lo_, hi_ in ((4, 0, 16), (7, 16, NB)):
                sp.wait_ge(s.pq_c, done)
                sp.dma_start(d_p.rearrange("(a p) f -> p a f", p=P)[:, lo_:hi_, :], PQ[:, lo_:hi_, 0:F]).then_inc(s.st_p, 16)
                sp.dma_start(d_q.rearrange("(a p) f -> p a f", p=P)[:, lo_:hi_, :], PQ[:, lo_:hi_, F:P]).then_inc(s.st_q, 16)
            sp.wait_ge(s.flag, 1)

            def superblock(r, i, h, b, k, kh, q, mb, qh, more):
                sp.wait_ge(r.add[b], h + 1)
                sp.dma_start(idx[:, b, :], rows(src, i)).then_inc(r.idx[b], 16)
                if r is R[0]:
                    base = sp.value_load(base_row[0:1, ds(i, 1)], min_val=0, max_val=N - 1)
                    sp.wait_ge(s.st_q, 32)
                    sp.wait_ge(r.pre[b], h + 1)
                    for half in range(2):
                        sp.dma_start(QD[(SPAN + 1) * half:(SPAN + 1) * half + SPAN, b, F * half:F * half + F],
                                     d_q[ds(base, SPAN), :]).then_inc(r.qd[b], 16)
                else:
                    sp.wait_ge(r.tr[b], h + 1)
                    sp.dma_start(EA[:, b, :], eattr.rearrange("(i p k) f -> i p (k f)", p=P, k=8)[ds(i, 1), :, :]
                                 .rearrange("o p e -> p (o e)")).then_inc(r.ea[b], 16)
                if k is not None:
                    sp.wait_ge(s.st_rows, 32)
                    sp.wait_ge(s.rec_c, 8)
                    for w in range(2):
                        lo = sp.value_load(lo_row[0:1, ds(2 * k + w, 1)], min_val=0, max_val=NT - TPW)
                        if w == 0:
                            sp.wait_ge(s.pair_v[b], kh + 1)
                        sp.dma_start(wrec[:, b, w * TPW:(w + 1) * TPW, :],
                                     rec[:, ds(lo, TPW), :]).then_inc(s.wrec[b], 16)

            def ordered0():
                edge_loop(sp, 0, superblock)
                sp.wait_ge(R[0].oh[0], 2 * (NSB // 2 + 1))
                sp.wait_ge(R[0].oh[1], 2 * (NSB // 2))
                sp.wait_ge(R[0].pre[0], NSB // 2 + 1 + 1)

            def general(r):
                with sp.Fori(0, NSB) as i:
                    sp.wait_ge(r.m_agg, (NCH + 1) * i + 1)
                    sp.dma_start(idx[:, 0, :], rows(src, i)).then_inc(r.m_ld, 16)
                    sp.dma_start(idx[:, 1, :], rows(dst, i)).then_inc(r.m_ld, 16)
                    if r is R[1]:
                        sp.dma_start(EA[:, 0, :], eattr.rearrange("(i p k) f -> i p (k f)", p=P, k=8)[ds(i, 1), :, :]
                                     .rearrange("o p e -> p (o e)")).then_inc(r.m_ld, 16)
                sp.wait_ge(r.m_agg, (NCH + 1) * NSB + 1)

            def general0():
                sp.wait_ge(s.gen_st, 16 * STR)
                for q in range(2):
                    sp.sem_inc(s.stg[q], 16 * (NQ // 2))
                sp.wait_ge(s.gen_clear, 1)
                sp.dma_start(w1c, W1_0[2 * F:2 * F + 1, :].to_broadcast([P, F])).then_inc(s.gen_w1c, 16)
                general(R[0])

            by_order(sp, general0, ordered0)
            sp.dma_start(ewall, ew.rearrange("(i p k) -> p i k", p=P, k=8)).then_inc(s.ld_w, 16)
            sp.wait_ge(s.nb_v, NB_WEBD)
            for j in range(4):
                sp.dma_start(WEBD[ED * j:ED * j + ED, F * j:F * j + F], We).then_inc(s.ld_we, 16)

            def ordered1():
                edge_loop(sp, 1, superblock)
            by_order(sp, lambda: general(R[1]), ordered1)
            sp.wait_ge(s.nc_v, 1)
            for o, i_ in ((w1n, W1_1), (w2n[0:F, 0:F], W2_1), (w2n[F:F + 1, 0:F], b2_1.rearrange("(o f) -> o f", o=1)),
                          (b1n, b1_1.rearrange("(f o) -> f o", o=1)),
                          (epsn, eps_gin.rearrange("(o k) -> o k", o=1).to_broadcast([P, 1])),
                          (gam, gamma.rearrange("(o f) -> o f", o=1).to_broadcast([P, F])),
                          (bet, beta.rearrange("(o f) -> o f", o=1).to_broadcast([P, F]))):
                sp.dma_start(o, i_).then_inc(s.ld_l1, 16)
            sp.wait_ge(s.stg[0], 16 * (NQ // 2) + 16)
            sp.wait_ge(s.stg[1], 16 * (NQ // 2) + 16)
            sp.wait_ge(s.nc_v, NC_X2)

            def load_piece(j):
                c, part = j // NPC, j % NPC
                sp.dma_start(ring[:, j % RING, :].rearrange("p (q e) -> p q e", q=CH // QC),
                             d_w[:, c * (CH // QC):(c + 1) * (CH // QC), part * PIECE:(part + 1) * PIECE, :]
                             .rearrange("p q a e -> p q (a e)")).then_inc(s.pc[j % RING], 16)

            def piece_used(k, j):
                c, part = j // NPC, j % NPC
                if part == NPC - 1:
                    sp.wait_ge(s.acc_t, NPOS * k + CORDER.index(c) + 1)
                else:
                    sp.wait_ge(s.pc_free, (NPC - 1) * (NCH * k + c) + part + 1)
            for j in range(RING):
                load_piece(j)
            for j in range(NPIECE):
                piece_used(0, j)
                sp.wait_ge(s.deg_v, j + 1 + (j >= NPC))
                load_piece((j + RING) % NPIECE)
            with sp.Fori(1, KTOT - 1) as k:
                for j in range(NPIECE):
                    piece_used(k, j)
                    load_piece((j + RING) % NPIECE)
            for j in range(NPIECE - RING):
                piece_used(KTOT - 1, j)
                load_piece(j + RING)
            sp.wait_ge(s.nd_v, ND_OUT)
            sp.dma_start(out[0:(NB - 1) * P, :].rearrange("(a p) f -> p a f", p=P), xs[0][:, 0:NB - 1, :]).then_inc(s.st_out, 16)
            sp.dma_start(out[(NB - 1) * P:N, :], xs[0][0:N - (NB - 1) * P, NB - 1, :]).then_inc(s.st_out, 16)
            sp.wait_ge(s.st_out, 32)

        @block.gpsimd
        def _(pool):
            g = nc.gpsimd
            g.iota(iota, pattern=[[1, P]], base=0, channel_multiplier=0, allow_small_or_imprecise_dtypes=True).then_inc(s.consts, 1)
            g.iota(tiota, pattern=[[1, NT]], base=0, channel_multiplier=0, allow_small_or_imprecise_dtypes=True).then_inc(s.consts, 1)
            g.iota(edge8[:, 0:4], pattern=[[WIN, 4]], base=0, channel_multiplier=4 * WIN, allow_small_or_imprecise_dtypes=True).then_inc(s.consts, 1)
            g.iota(edge8[:, 4:8], pattern=[[WIN, 4]], base=WIN - 1, channel_multiplier=4 * WIN, allow_small_or_imprecise_dtypes=True).then_inc(s.consts, 1)
            g.memset(ident, 0.0).then_inc(s.consts, 1)
            g.memset(at(o_qd, 2, P), 0.0).then_inc(s.consts, 1)
            g.memset(aggT, 0.0).then_inc(s.consts, 1)
            g.memset(ones, 1.0).then_inc(s.consts, 1)
            g.iota(wcols0, pattern=[[1, PAIR]], base=-PAIR, channel_multiplier=0, allow_small_or_imprecise_dtypes=True).then_inc(s.consts, 1)
            pool.wait_ge(s.consts, C_FIRST)
            g.affine_select(out=ident, in_=ident, compare_op=ALU.not_equal, fill=1.0, base=0,
                            pattern=[[-1, P]], channel_multiplier=1).then_inc(s.consts, 1)

            def superblock(r, i, h, b, k, kh, q, mb, qh, more):
                table = d_p if r is R[0] else d_t1
                pool.wait_ge(r.idx[b], 16 * (h + 1))
                pool.wait_ge(r.seg[b], h + 1)
                pool.nop(nofuse=True)
                for j in range(8):
                    g.indirect_dma_start(G[:, b, j, :], None, table,
                                         bass.IndirectOffsetOnAxis(ap=idx[:, b, j:j + 1], axis=0)).then_inc(r.g[b], 16)

            pool.wait_ge(s.ld_bc, 48)
            g.tensor_tensor(bad[:, 0, 0:NT - 1], tmaxB[0:1, 0:NT - 1], tminB[0:1, 1:NT], ALU.subtract).then_inc(s.bad, 1)
            g.tensor_tensor(bad[:, 1, 0:NT - TPW], tmaxB[0:1, 0:NT - TPW], tminB[0:1, TPW:NT], ALU.subtract).then_inc(s.bad, 1)
            g.tensor_tensor(bad[:, 2, 0:NSB], tmaxB[0:1, :].rearrange("p (i k) -> p i k", k=8)[:, :, 7], bB[0:1, :], ALU.subtract).then_inc(s.bad, 1)
            pool.wait_ge(s.flag, 1)

            def general(r):
                with pool.Fori(0, NSB) as i:
                    pool.wait_ge(r.m_ld, 16 * (2 if r is R[0] else 3) * (i + 1))
                    pool.wait_ge(r.m_dst, i + 1)
                    pool.nop(nofuse=True)
                    for j in range(8):
                        g.indirect_dma_start(G[:, 0, j, :], None, d_p if r is R[0] else d_t1,
                                             bass.IndirectOffsetOnAxis(ap=idx[:, 0, j:j + 1], axis=0)).then_inc(r.m_g, 16)
                    if r is R[0]:
                        for j in range(8):
                            g.indirect_dma_start(G[:, 1, j, :], None, d_q,
                                                 bass.IndirectOffsetOnAxis(ap=idx[:, 1, j:j + 1], axis=0)).then_inc(r.m_g, 16)

            def general0():
                pool.wait_ge(s.st_q, 32)
                g.iota(iotaW, pattern=[[1, NP]], base=0, channel_multiplier=0, allow_small_or_imprecise_dtypes=True).then_inc(s.gen_iota, 1)
                general(R[0])

            pool.wait_ge(s.st_p, 32)
            by_order(pool, general0, lambda: edge_loop(pool, 0, superblock))
            pool.wait_ge(s.st_t1, 16)
            by_order(pool, lambda: general(R[1]), lambda: edge_loop(pool, 1, superblock))

        @block.vector
        def _(v):
            d = nc.vector
            start_rings(v, [s.pair_v, [s.pair_step]] + [x for r in R for x in (r.agg, r.add, [r.m_agg])])
            V_IN = [0]

            def prep(ins):
                V_IN[0] += 1
                ins.then_inc(s.prep_v, 1)
                v.wait_ge(s.prep_v, V_IN[0])
            d.memset(xT[F:F + 1, :], 1.0).then_inc(s.consts, 1)
            d.memset(w1ab, 0.0).then_inc(s.consts, 1)
            d.memset(w2p, 0.0).then_inc(s.consts, 1)
            v.wait_ge(s.ld_edges, 48)
            prep(d.tensor_copy(fld[2], dstN))
            prep(d.tensor_reduce(tmin, fld[2].rearrange("p (k e) -> p k e", e=P), AX, ALU.min))
            prep(d.tensor_reduce(tmax, fld[2].rearrange("p (k e) -> p k e", e=P), AX, ALU.max))
            prep(d.tensor_scalar(tmax, tmax, float(N - 1), None, ALU.min))
            prep(d.tensor_reduce(bmin, tmin, AX, ALU.min))
            prep(d.tensor_scalar(srcI[0], srcN, P - 1, None, ALU.bitwise_and))
            prep(d.tensor_scalar(srcI[1], srcN, 7, None, ALU.logical_shift_right))
            prep(d.tensor_copy(fld[0], srcI[0]))
            prep(d.tensor_copy(fld[1], srcI[1]))
            assert V_IN[0] == V_FLD
            v.wait_ge(s.ld_bc, 48)
            prep(d.tensor_copy(base_row, bB[0:1, :]))
            v.wait_ge(s.bad, 3)
            for j, (n, bound) in enumerate(((NT - 1, 0), (NT - TPW, -WIN), (NSB, SPAN - 1))):
                prep(d.tensor_reduce(worst[:, j:j + 1], bad[:, j, 0:n], AX, ALU.max))
                prep(d.tensor_scalar(worst[:, j:j + 1], worst[:, j:j + 1], float(-bound), None, ALU.add))
            prep(d.tensor_reduce(worst[:, 0:1], worst, AX, ALU.max))
            d.tensor_scalar(flag, worst[:, 0:1], 0.0, None, ALU.is_gt).then_inc(s.flag, 1)
            v.wait_ge(s.flag, 1)
            v.wait_ge(s.consts, C_FIRST)
            for q in range(4):
                prep(d.tensor_scalar(c1, tminB[0:WQ, :], edge8[:, 4 + q:5 + q], None, ALU.is_le))
                prep(d.scalar_tensor_tensor(c1, tmaxB[0:WQ, :], edge8[:, q:q + 1], c1, ALU.is_ge, ALU.mult))
                prep(d.scalar_tensor_tensor(c2, c1, -4096.0, tiota[0:WQ, :], ALU.mult, ALU.add))
                prep(d.tensor_reduce(lohi[:, q:q + 1], c2, AX, ALU.min))
            prep(d.tensor_scalar(lo_i, lohi[:, 0:4], 4096.0, float(NT - TPW), ALU.add, ALU.min))
            assert V_IN[0] == V_ROWS
            v.wait_ge(s.ld_sb, 32)
            prep(d.tensor_tensor(rel.rearrange("p (i k) -> p i k", k=8), dstS, bB.unsqueeze(2).to_broadcast([P, NSB, 8]), ALU.subtract))

            v.wait_ge(s.consts, C_ALL)

            def one_hots(r, i, h, b):
                v.wait_ge(r.seg[b], h + 1)
                d.tensor_tensor(OH[:, b, :, 0:SPAN],
                                rel[:, ds(8 * i, 8)].unsqueeze(2).to_broadcast([P, 8, SPAN]),
                                iota[:, 0:SPAN].unsqueeze(1).to_broadcast([P, 8, SPAN]), ALU.is_equal).then_inc(r.oh[b], 1)
                d.tensor_copy(OH[:, b][:, :, SPAN:SPAN + 1],
                              ewflat[:, ds(8 * i, 8)].unsqueeze(2)).then_inc(r.oh[b], 1)

            def pair_low(k, kh, b):
                v.wait_ge(s.wrec[b], 32 * (kh + 1))
                v.wait_ge(s.pair_t[b], kh + 1)
                w_ = wrec[:, b]
                bc = lambda f, n: w_[:, :, f:f + 1].to_broadcast([P, 2 * TPW, n])
                hp, bp = following(kh, b)
                v.wait_ge(s.pair_v[bp], hp + 1)
                v.wait_ge(s.pair_step, 5 * k + 1)
                d.tensor_scalar(wcols, wcols, float(PAIR), None, ALU.add).then_inc(s.pair_step, 1)
                d.tensor_tensor(alo[:, b], bc(0, P), iota.unsqueeze(1).to_broadcast([P, 2 * TPW, P]), ALU.is_equal).then_inc(s.pair_step, 1)
                d.tensor_tensor(hi1, bc(1, NB), iota[:, 0:NB].unsqueeze(1).to_broadcast([P, 2 * TPW, NB]), ALU.is_equal).then_inc(s.pair_step, 1)

            def pair_outer(k, kh, b):
                w_ = wrec[:, b]
                bc = lambda f, n: w_[:, :, f:f + 1].to_broadcast([P, 2 * TPW, n])
                v.wait_ge(s.pair_step, 5 * k + 1 + 1)
                d.tensor_tensor(dsel.rearrange("p (w t) j -> p w t j", w=2),
                                w_[:, :, 2:3].rearrange("p (w t) o -> p w t o", w=2).to_broadcast([P, 2, TPW, WIN]),
                                wcols.rearrange("p (w j) -> p w j", w=2).unsqueeze(2).to_broadcast([P, 2, TPW, WIN]),
                                ALU.is_equal).then_inc(s.pair_step, 1)
                v.wait_ge(s.pair_step, 5 * k + 4 + 1)
                d.tensor_tensor(dsel, dsel, bc(3, WIN), ALU.mult).then_inc(s.pair_step, 1)
                v.wait_ge(s.pair_step, 5 * k + 5 + 1)
                d.tensor_tensor(outer[:, b].rearrange("p t (c j) -> p t c j", j=WIN),
                                hi1.unsqueeze(3).to_broadcast([P, 2 * TPW, NB, WIN]),
                                dsel.unsqueeze(2).to_broadcast([P, 2 * TPW, NB, WIN]), ALU.mult).then_inc(s.pair_v[b], 1)

            def superblock(r, i, h, b, k, kh, q, mb, qh, more):
                base = v.value_load(base_row[0:1, ds(i, 1)], min_val=0, max_val=N - 1)
                if k is not None:
                    pair_low(k, kh, b)
                v.wait_ge(r.pre[b], h + 1 + 1)
                v.wait_ge(r.g[b], P * (h + 1))
                gflat = G[:, b].rearrange("p k f -> p (k f)")
                d.tensor_tensor(gflat, psPre[b][:, :], gflat, ALU.add).then_inc(r.add[b], 1)
                hn, bn = following(h, b)
                if more:
                    one_hots(r, i + 1, hn, bn)
                if k is not None:
                    pair_outer(k, kh, b)
                v.wait_ge(r.seg[b], h + 1 + 1)
                v.wait_ge(r.agg[bn], hn + 1)
                cols = aggT[:, ds(base, SPAN)]
                d.tensor_tensor(cols, psSeg[:, P * b:P * b + SPAN], cols, ALU.add).then_inc(r.agg[b], 1)

            def ordered0():
                prep(d.tensor_copy(wcols, wcols0))
                one_hots(R[0], 0, 0, 0)
                edge_loop(v, 0, superblock)

            def gen_block(n, resident):
                steps = 2 * NT + 1
                v.wait_ge(s.gen_step, steps * n + 1)
                d.tensor_scalar(gen_n, gen_n, 1.0, None, ALU.add).then_inc(s.gen_step, 1)
                with v.Fori(0, NT // 2) as h:
                    for b in range(2):
                        v.wait_ge(s.gen_mm[b], NT // 2 * n + h + 1)
                        d.tensor_tensor(genB[b], iotaW[:, 0:NCOL], rec[:, ds(2 * h + b, 1), 2].to_broadcast([P, NCOL]),
                                        ALU.is_equal).then_inc(s.gen_op[b], 1)
                        v.wait_ge(s.gen_step, steps * n + 4 * h + (2 * b + 2))
                        d.tensor_copy(gen_cur[b], rec[:, ds(2 * h + b, 1), :].rearrange("p o f -> p (o f)")).then_inc(s.gen_step, 1)
                        v.wait_ge(s.gen_step, steps * n + 4 * h + (2 * b + 3))
                        d.scalar_tensor_tensor(gen_wn[b], gen_cur[b][:, 1:2], gen_n, gen_cur[b][:, 3:4], ALU.is_equal, ALU.mult).then_inc(s.gen_step, 1)
                        v.wait_ge(s.gen_step, steps * n + 4 * h + (2 * b + 4))
                        d.tensor_scalar(genA[b], iota, gen_cur[b][:, 0:1], gen_wn[b], ALU.is_equal, ALU.mult).then_inc(s.gen_op[b], 1)

            def general(r):
                steps = 5 if r is R[0] else 3
                with v.Fori(0, NSB) as i:
                    v.wait_ge(r.m_ld, 16 * (2 if r is R[0] else 3) * (i + 1))
                    v.wait_ge(r.m_agg, (NCH + 1) * i + 1)
                    d.tensor_copy(dcol, idx[:, 1, :]).then_inc(r.m_step, 1)
                    d.tensor_copy(wcol, ewflat[:, ds(8 * i, 8)]).then_inc(r.m_step, 1)
                    d.tensor_scalar(idx[:, 1, :], idx[:, 1, :], NP - 1, None, ALU.min).then_inc(r.m_dst, 1)
                    v.wait_ge(r.m_g, P * (2 if r is R[0] else 1) * (i + 1))
                    g0, g1 = G[:, 0], G[:, 1]
                    if r is R[0]:
                        d.tensor_tensor(g0, g0, g1, ALU.add).then_inc(r.m_step, 1)
                        v.wait_ge(r.m_step, steps * i + 3)
                        d.tensor_tensor(g1, w1c.unsqueeze(1).to_broadcast([P, 8, F]), wcol.unsqueeze(2).to_broadcast([P, 8, F]), ALU.mult).then_inc(r.m_step, 1)
                        v.wait_ge(r.m_step, steps * i + 4)
                        d.tensor_tensor(g0, g0, g1, ALU.add).then_inc(r.m_step, 1)
                    else:
                        v.wait_ge(r.m_pre, i + 1)
                        gflat = g0.rearrange("p k f -> p (k f)")
                        d.tensor_tensor(gflat, psPre[0][:, :], gflat, ALU.add).then_inc(r.m_step, 1)
                    v.wait_ge(r.m_step, steps * i + steps)
                    d.tensor_scalar(g0, g0, 0.0, None, ALU.max).then_inc(r.m_msg, 1)

                    def chunk(c, w_):
                        for k in range(8):
                            v.wait_ge(r.m_mm[k % 2], 4 * (NCH + 1) * i + 4 * c + (k // 2 + 1))
                            d.tensor_tensor(genOH[k % 2][:, 0:w_], iotaW[:, ds(CH * c, w_)], dcol[:, k:k + 1].to_broadcast([P, w_]),
                                            ALU.is_equal).then_inc(r.m_oh[k % 2], 1)
                        for b in range(2):
                            v.wait_ge(r.m_mm[b], 4 * (NCH + 1) * i + 4 * c + 5)
                        v.wait_ge(r.m_agg, (NCH + 1) * i + c + 1)
                        d.tensor_tensor(aggT[:, ds(CH * c, w_)], psSeg[:, 0:w_], aggT[:, ds(CH * c, w_)], ALU.add).then_inc(r.m_agg, 1)
                    chunks(v, chunk)
                v.wait_ge(r.m_agg, (NCH + 1) * NSB + 1)

            def general0():
                v.wait_ge(s.gen_iota, 1)
                v.wait_ge(s.rec_c, 8)
                v.wait_ge(s.ld_wts, WTS)
                d.memset(gen_n, -1.0).then_inc(s.gen_step, 1)
                blocks(v, gen_block)
                for b in range(2):
                    v.wait_ge(s.gen_mm[b], NB * (NT // 2) + 1)
                v.wait_ge(s.gen_st, 16 * STR)
                d.memset(aggT, 0.0).then_inc(s.gen_clear, 1)
                v.wait_ge(s.gen_clear, 1)
                v.wait_ge(s.gen_w1c, 16)
                general(R[0])

            by_order(v, general0, ordered0)

            cnt = [0]

            def link(ins, name=None):
                cnt[0] += 1
                ins.then_inc(s.nb_v, 1)
                v.wait_ge(s.nb_v, cnt[0])

            def norm(link_, a_sem, a_at, y, tmp_, sc, out_):
                link_(d.tensor_reduce(sc[:, 0, :], y, AX, ALU.add))
                link_(d.tensor_scalar(sc[:, 1, :], sc[:, 0, :], -1.0 / F, None, ALU.mult))
                link_(d.tensor_tensor(y, y, sc[:, 1, :].unsqueeze(2).to_broadcast([P, NB, F]), ALU.add))
                v.wait_ge(a_sem, a_at)
                link_(d.tensor_reduce(sc[:, 2, :], tmp_, AX, ALU.add))
                link_(d.tensor_scalar(sc[:, 3, :], sc[:, 2, :], 1.0 / F, EPS, ALU.mult, ALU.add))
                v.wait_ge(a_sem, a_at + 1)
                link_(d.reciprocal(sc[:, 5, :], sc[:, 4, :]))
                link_(d.tensor_tensor(out_, y, sc[:, 5, :].unsqueeze(2).to_broadcast([P, NB, F]), ALU.mult))

            for g5 in range(5):
                v.wait_ge(s.nb_t, g5 + 1)
                link(d.tensor_tensor(lnA[:, 5 * g5:5 * g5 + 5, :], banks[g5][:, 0:5 * HALF].rearrange("p (a c) -> p a c", c=HALF)[:, :, 0:F],
                                     xa[:, 5 * g5:5 * g5 + 5, :], ALU.add))
            norm(link, s.nb_a, 1, lnA, lnB, lnS, xa)
            v.wait_ge(s.ld_wts, WTS)
            assert cnt[0] == NB_X1
            link(d.tensor_tensor(lnB, xa, beB.unsqueeze(1).to_broadcast([P, NB, F]), ALU.add))
            link(d.memset(aggT, 0.0))
            link(d.memset(WEBD, 0.0))
            assert cnt[0] == NB_WEBD
            v.wait_ge(s.ld_w, 16)
            v.wait_ge(s.st_t1, 16)

            def ordered1():
                one_hots(R[1], 0, 0, 0)
                edge_loop(v, 1, superblock)
            by_order(v, lambda: general(R[1]), ordered1)

            cnt[0] = 0

            def link2(ins):
                cnt[0] += 1
                ins.then_inc(s.nc_v, 1)
                v.wait_ge(s.nc_v, cnt[0])
            link2(d.memset(at(o_l1, 4 * F + 3 * HALF), 0.0))
            v.wait_ge(s.ld_l1, 7 * 16)
            link2(d.tensor_scalar(epsn, epsn, 1.0, None, ALU.add))
            link2(d.memset(sel[F:F + 1, 0:1], 1.0))
            link2(d.memset(h1T[F:F + 1, :], 1.0))
            v.wait_ge(s.stg[0], 16 * (NQ // 2) + 16)
            v.wait_ge(s.stg[1], 16 * (NQ // 2) + 16)
            for g4 in range(7):
                w_ = min(CH, NP - CH * g4)
                v.wait_ge(s.nc_t, g4 + 1)
                link2(d.scalar_tensor_tensor(hT[0:F, CH * g4:CH * g4 + w_], banks[g4][0:F, 0:w_], epsn[0:F, :],
                                             aggT[0:F, CH * g4:CH * g4 + w_], ALU.mult, ALU.add))
            assert cnt[0] == NC_HT
            v.wait_ge(s.nc_t, NCT_DEG)
            for g5 in range(5):
                link2(d.tensor_copy(nsc[:, 0, 5 * g5:5 * g5 + 5],
                                    banks[DEGB[g5]][:, 0:5 * HALF].rearrange("p (a c) -> p a c", c=HALF)[:, :, 0]))
            link2(d.tensor_scalar(nsc[:, 2, :], nsc[:, 0, :], 1.0, None, ALU.add))
            link2(d.tensor_scalar(nsc[:, 4, :], nsc[:, 0, :], TINY, None, ALU.max))
            link2(d.tensor_scalar(nsc[:, 5, :], nsc[:, 2, :], TINY, None, ALU.max))
            assert cnt[0] == NC_DEG
            v.wait_ge(s.nc_a, NCA_ROOT)
            link2(d.reciprocal(nsc[:, 4:6, :], nsc[:, 7:9, :]))
            link2(d.scalar_tensor_tensor(nsc[:, 7, :], nsc[:, 0, :], 0.0, nsc[:, 4, :], ALU.is_gt, ALU.mult))
            link2(d.scalar_tensor_tensor(nsc[:, 8, :], nsc[:, 2, :], 0.0, nsc[:, 5, :], ALU.is_gt, ALU.mult))
            link2(d.tensor_scalar(nsc[:, 10, :], nsc[:, 8, :], 1.0 - ALPHA, None, ALU.mult))
            dinv, dout, a_last, a_mid = nsc[:, 7, :], nsc[:, 9, :], nsc[:, 10, :], nsc[:, 11, :]
            v.wait_ge(s.nc_a, NCA_H2)
            link2(d.scalar_tensor_tensor(lnA, lnA, 0.2, lnA, ALU.mult, ALU.max))
            assert cnt[0] == NC_LEAKY
            norm(link2, s.nc_a, NCA_ROOT + 1, lnA, lnB, lnS, lnB)
            link2(d.tensor_tensor(lnB, lnB, gam.unsqueeze(1).to_broadcast([P, NB, F]), ALU.mult))
            link2(d.tensor_tensor(lnB, lnB, bet.unsqueeze(1).to_broadcast([P, NB, F]), ALU.add))
            link2(d.tensor_tensor(lnA, lnB, xa, ALU.add))
            norm(link2, s.nc_a, NCA_ROOT + 3, lnA, lnB, lnS, x2)
            assert cnt[0] == NC_X2, cnt[0]
            v.wait_ge(s.ld_lw, 16)

            cnt[0] = 0

            def link3(ins):
                cnt[0] += 1
                ins.then_inc(s.nd_v, 1)
                v.wait_ge(s.nd_v, cnt[0])

            def by_node(col, lo_=0, n=NB):
                return col[:, lo_:lo_ + n].unsqueeze(2).to_broadcast([P, n, F])
            link3(d.tensor_tensor(xs[0], x2, by_node(dinv), ALU.mult))
            link3(d.tensor_reduce(lwt[:, 4:5], lwt[:, 0:4], AX, ALU.max))
            link3(d.tensor_scalar(lwt[:, 5:6], lwt[:, 4:5], -1.0, None, ALU.mult))
            v.wait_ge(s.nd_a, 1)
            link3(d.tensor_reduce(lwt[:, 10:11], lwt[:, 6:10], AX, ALU.add))
            link3(d.reciprocal(lwt[:, 11:12], lwt[:, 10:11]))
            link3(d.tensor_scalar(lwt[:, 12:16], lwt[:, 6:10], lwt[:, 11:12], None, ALU.mult))
            link3(d.tensor_scalar(comb.rearrange("p a f -> p (a f)"), x2.rearrange("p a f -> p (a f)"), lwt[:, 12:13], None, ALU.mult))
            assert cnt[0] == ND_L2

            def sums(k, c):
                if not isinstance(k, int):
                    return
                if k == 0 and c == NCH:
                    d.tensor_reduce(deg_str[:, c, :], W6, AX, ALU.add).then_inc(s.deg_v, 1)
                elif k == 0:
                    for j in range(NPC * c, NPC * c + NPC):
                        v.wait_ge(s.pc[j % RING], 16 * (j // RING + 1))
                        part = (j % NPC) * PIECE
                        d.tensor_reduce(deg_str[:, c, part:part + PIECE],
                                        ring[:, j % RING, :].rearrange("p (q a e) -> p a q e", q=CH // QC, e=QC),
                                        mybir.AxisListType.XY, ALU.add).then_inc(s.deg_v, 1)
                elif k == 1:
                    for n in range(RES * CORDER.index(c) // NPOS, RES * (CORDER.index(c) + 1) // NPOS):
                        d.tensor_reduce(nsc[:, 1, n:n + 1], Wres[:, n, :], AX, ALU.add).then_inc(s.deg_v, 1)

            def post_chunks(k, old, new, steps):
                for t_, c in enumerate(CORDER):
                    n = 4 if c < NCH else 1
                    lo_ = 4 * c
                    sums(k, c)
                    v.wait_ge(s.out_t, NPOS * k + t_ + 1)
                    prod = banks[4 + t_ % 4][:, 0:n * P].rearrange("p (a c) -> p a c", c=P)
                    y = post[:, 0:n, :]
                    if t_ or not isinstance(k, int) or k:
                        v.wait_ge(s.comb_v if steps is step2 else s.xs_v, NPOS * k + t_)
                    if steps is step2:
                        d.tensor_copy(y, prod[:, :, 0:F]).then_inc(s.post_v, 1)
                    else:
                        d.tensor_tensor(y, prod[:, :, 0:F], old[:, lo_:lo_ + n, :], ALU.add).then_inc(s.post_v, 1)
                    v.wait_ge(s.post_v, 3 * (NPOS * k + t_) + 1)
                    d.tensor_tensor(y, prod[:, :, F:P], y, ALU.add).then_inc(s.post_v, 1)
                    v.wait_ge(s.post_v, 3 * (NPOS * k + t_) + 2)
                    steps(k, t_, lo_, n, y, old, new)

            def step2(k, t_, lo_, n, y, old, new):
                d.tensor_tensor(y, y, by_node(dinv, lo_, n), ALU.mult).then_inc(s.post_v, 1)
                v.wait_ge(s.post_v, 3 * (NPOS * k + t_) + 3)
                d.tensor_tensor(new[:, lo_:lo_ + n, :], y, by_node(dinv, lo_, n), ALU.mult).then_inc(s.xs_v, 1)
                cb = comb[:, lo_:lo_ + n, :]
                d.scalar_tensor_tensor(cb, y, lwt[:, 13 + k:14 + k], cb, ALU.mult, ALU.add).then_inc(s.comb_v, 1)

            def step3(a):
                def step(k, t_, lo_, n, y, old, new):
                    d.tensor_tensor(y, y, by_node(a, lo_, n), ALU.mult).then_inc(s.post_v, 1)
                    v.wait_ge(s.post_v, 3 * (NPOS * k + t_) + 3)
                    d.tensor_tensor(new[:, lo_:lo_ + n, :], y, gb[:, lo_:lo_ + n, :], ALU.add).then_inc(s.xs_v, 1)
                return step

            for k in range(K2):
                post_chunks(k, xs[k % 2], xs[(k + 1) % 2], step2)
            v.wait_ge(s.comb_v, NPOS * K2)
            v.wait_ge(s.deg_v, NPIECE + 1 + RES)
            link3(d.tensor_reduce(nsc[:, 1, RES:NB], deg_str.rearrange("p c n -> p n c"), AX, ALU.add))
            link3(d.tensor_scalar(nsc[:, 3, :], nsc[:, 1, :], 1.0, None, ALU.add))
            link3(d.tensor_scalar(nsc[:, 6, :], nsc[:, 3, :], TINY, None, ALU.max))
            assert cnt[0] == ND_DOUT
            v.wait_ge(s.nd_a, 3)
            link3(d.reciprocal(nsc[:, 6, :], nsc[:, 9, :]))
            link3(d.scalar_tensor_tensor(nsc[:, 9, :], nsc[:, 3, :], 0.0, nsc[:, 6, :], ALU.is_gt, ALU.mult))
            link3(d.tensor_tensor(nsc[:, 11, :], nsc[:, 10, :], nsc[:, 9, :], ALU.mult))
            link3(d.tensor_reduce(nsc[:, 0, :], gb, AX, ALU.add))
            v.wait_ge(s.nd_a, 4)
            link3(d.tensor_scalar(nsc[:, 1, :], nsc[:, 1, :], 1e-12, None, ALU.max))
            link3(d.reciprocal(nsc[:, 2, :], nsc[:, 1, :]))
            link3(d.tensor_tensor(comb, comb, by_node(nsc[:, 2, :]), ALU.mult))
            link3(d.tensor_tensor(comb, comb, x2, ALU.add))
            assert cnt[0] == ND_LN2
            norm(link3, s.nd_a, 5, comb, gb, nsc, x2)
            link3(d.tensor_tensor(xs[1], x2, by_node(dout), ALU.mult))
            link3(d.tensor_scalar(gb.rearrange("p a f -> p (a f)"), xs[1].rearrange("p a f -> p (a f)"), ALPHA, None, ALU.mult))
            assert cnt[0] == ND_L3
            with v.Fori(0, (K3 - 2) // 2) as kk:
                for par in range(2):
                    post_chunks(2 * kk + (K2 + par), xs[(1 + par) % 2], xs[par % 2], step3(a_mid))
            post_chunks(KTOT - 2, xs[1], xs[0], step3(a_mid))
            v.wait_ge(s.xs_v, NPOS * (KTOT - 1))
            link3(d.tensor_scalar(gb.rearrange("p a f -> p (a f)"), x2.rearrange("p a f -> p (a f)"), ALPHA, None, ALU.mult))
            post_chunks(KTOT - 1, xs[0], xs[1], step3(a_last))
            v.wait_ge(s.xs_v, NPOS * KTOT)
            link3(d.tensor_tensor(comb, xs[1], x2, ALU.add))
            assert cnt[0] == ND_LN3, cnt[0]
            norm(link3, s.nd_a, 7, comb, gb, nsc, xs[0])
            assert cnt[0] == ND_OUT, cnt[0]

        @block.scalar
        def _(act):
            a = nc.scalar
            start_rings(act, [s.pair_e, [s.gen_out]])
            for q in range(2):
                act.dma_start(first2[0:1, q:q + 1], lw[0:1].rearrange("(o k) -> o k", o=1)).then_inc(s.stg[q], 16)
            act.dma_start(xa, x.rearrange("(a p) f -> p a f", p=P)).then_inc(s.ld_x, 16)
            act.dma_start(beB, be.rearrange("(o f) -> o f", o=1).to_broadcast([P, F])).then_inc(s.ld_wts, 16)
            act.wait_ge(s.consts, C_FIRST)
            act.dma_start(w1ab[0:F, 0:F], W1_0[0:F, :]).then_inc(s.ld_wts, 16)
            act.dma_start(w1ab[0:F, F:P], W1_0[F:2 * F, :]).then_inc(s.ld_wts, 16)
            act.dma_start(w2p[0:F, 0:F], W2_0).then_inc(s.ld_wts, 16)
            act.dma_start(w2p[F:F + 1, 0:F], b2_0.rearrange("(o f) -> o f", o=1)).then_inc(s.ld_wts, 16)
            act.dma_start(w1ab[F:F + 1, F:P], b1_0.rearrange("(o f) -> o f", o=1)).then_inc(s.ld_wts, 16)
            for b in range(2):
                for half in range(2):
                    row = (SPAN + 1) * half + SPAN
                    act.dma_start(QD[row:row + 1, b, F * half:F * half + F], W1_0[2 * F:2 * F + 1, :]).then_inc(s.ld_wts, 16)
            for g4 in range(7):
                w_ = min(CH, NP - CH * g4)
                act.wait_ge(s.xt_t, g4 + 1)
                a.activation(xT[0:F, CH * g4:CH * g4 + w_], banks[6 + g4 % 2][0:F, 0:w_], ACT.Copy).then_inc(s.xt_c, 1)
            for g4 in range(7):
                n = min(4, NB - 4 * g4)
                act.wait_ge(s.pq_t, g4 + 1)
                a.activation(PQ[:, 4 * g4:4 * g4 + n, :].rearrange("p a f -> p (a f)"), banks[2 + g4 % 2][:, 0:P * n], ACT.Copy).then_inc(s.pq_c, 1)
            recv = rec.rearrange("p (i j) f -> p i j f", j=8)
            for j in range(8):
                act.wait_ge(s.rec_t, j + 1)
                a.activation(recv[:, :, j, :], banks[j % 2][:, 0:4 * NSB].rearrange("p (f i) -> p i f", f=4), ACT.Copy).then_inc(s.rec_c, 1)

            def product_copy(r, h, b):
                act.wait_ge(r.tr[b], h + 1 + 1)
                act.wait_ge(r.pre[b], h + 1)
                if r is R[0]:
                    a.activation(OHT[:, b, :], psT[0:2 * (SPAN + 1), :], ACT.Copy).then_inc(r.trc[b], 1)
                else:
                    a.activation(EAT[:, b, :], psT[:, 0:2 * P], ACT.Copy).then_inc(r.trc[b], 1)

            def superblock(r, i, h, b, k, kh, q, mb, qh, more):
                act.wait_ge(r.add[b], h + 1 + 1)
                gflat = G[:, b].rearrange("p k f -> p (k f)")
                a.activation(gflat, gflat, ACT.Relu).then_inc(r.relu[b], 1)
                hn, bn = following(h, b)
                if more:
                    product_copy(r, hn, bn)
                if k is not None:
                    act.wait_ge(s.pair_t[b], kh + 1 + 1)
                    prod = psW[b].rearrange("p (c j) -> p c j", j=PAIR)
                    if q is not None:
                        act.wait_ge(s.stg[q], 16 * qh + 16)
                        a.activation(Wres[:, :, ds(PAIR * k, PAIR)], prod[:, 0:RES, :], ACT.Copy).then_inc(s.pair_e[b], 1)
                        a.activation(stage[:, q, :, ds(PAIR * mb, PAIR)], prod[:, RES:NB, :], ACT.Copy).then_inc(s.pair_e[b], 1)
                    else:
                        a.activation(Wres[:, :, PAIR * k:PAIR * k + PAIR], prod[:, 0:RES, :], ACT.Copy).then_inc(s.pair_e[b], 1)
                        a.activation(W6[:, :, PAIR * mb:PAIR * mb + PAIR], prod[:, RES:NB, :], ACT.Copy).then_inc(s.pair_e[b], 1)

            def quarter_end(Q, q, qh):
                if q is None:
                    return
                act.wait_ge(s.pair_e[0], 8 * Q + 8 + 1)
                act.wait_ge(s.pair_e[1], 8 * Q + 8 + 1)
                act.dma_start(d_w[:, ds(Q, 1), :, :].rearrange("p o a e -> p o (a e)"),
                              stage[:, q:q + 1, :, :].rearrange("p o a e -> p o (a e)")).then_inc(s.stg[q], 16)

            def norm(v_sem, v_at, y, tmp_, sc, a_sem):
                act.wait_ge(v_sem, v_at)
                a.activation(tmp_, y, ACT.Square).then_inc(a_sem, 1)
                act.wait_ge(v_sem, v_at + 2)
                a.activation(sc[:, 4, :], sc[:, 3, :], ACT.Sqrt).then_inc(a_sem, 1)

            def ordered(layer):
                product_copy(R[layer], 0, 0)
                edge_loop(act, layer, superblock, quarter_end)

            def gen_block(n, resident):
                for b in range(2):
                    act.wait_ge(s.gen_mm[b], NT // 2 * n + (NT // 2 + 1))
                for c in range(NCH + 1):
                    if resident:
                        w_ = CH if c < NCH else LASTW
                        to = Wres[:, ds(n, 1), CH * c:CH * c + w_].rearrange("p o e -> p (o e)")
                        a.activation(to, banks[c][:, 0:w_], ACT.Copy).then_inc(s.gen_out, 1)
                    elif c < NCH:
                        a.activation(gen_row[:, CH * c:CH * c + CH], banks[c][:, :], ACT.Copy).then_inc(s.gen_out, 1)
                    else:
                        a.activation(W6[:, ds(n - RES, 1), :].rearrange("p o e -> p (o e)"), banks[c][:, 0:LASTW], ACT.Copy).then_inc(s.gen_out, 1)
                if not resident:
                    act.wait_ge(s.gen_out, (NCH + 1) * (n + 1) + 1)
                    act.dma_start(d_w[:, :, ds(n - RES, 1), :].rearrange("p q o e -> p q (o e)"),
                                  gen_row.rearrange("p (q e) -> p q e", e=QC)).then_inc(s.gen_st, 16)
                    act.wait_ge(s.gen_st, 16 * (n - RES + 1))

            def general0():
                act.wait_ge(s.st_p, 32)
                act.wait_ge(s.st_q, 32)
                blocks(act, gen_block)

            def general1():
                with act.Fori(0, NSB) as i:
                    act.wait_ge(R[1].m_tr, i + 1)
                    a.activation(EAT[:, 0, :], psT[:, 0:2 * P], ACT.Copy).then_inc(R[1].m_trc, 1)

            act.wait_ge(s.prep_v, V_ROWS)
            act.dma_start(d_lo.rearrange("o (p k) -> p (o k)", k=4), lo_i).then_inc(s.st_rows, 16)
            act.wait_ge(s.st_rows, 16)
            act.dma_start(lo_row, d_lo).then_inc(s.st_rows, 16)
            act.wait_ge(s.st_rows, 32)
            act.wait_ge(s.flag, 1)
            by_order(act, general0, lambda: ordered(0))
            norm(s.nb_v, NB_Y + 3, lnA, lnB, lnS, s.nb_a)
            act.wait_ge(s.nb_v, NB_X1 + 1)
            act.dma_start(d_t1.rearrange("(a p) f -> p a f", p=P), lnB).then_inc(s.st_t1, 16)
            by_order(act, general1, lambda: ordered(1))
            act.wait_ge(s.ld_l1, 7 * 16)
            act.wait_ge(s.nc_v, 4)
            for g4 in range(7):
                w_ = min(CH, NP - CH * g4)
                act.wait_ge(s.nc_t, NCT_X1 + g4 + 1)
                a.activation(h1T[0:F, CH * g4:CH * g4 + w_], banks[(4 + g4) % 7][0:F, 0:w_], ACT.Relu, bias=b1n).then_inc(s.nc_a, 1)
            for g5 in range(5):
                act.wait_ge(s.nc_t, NCT_H1 + g5 + 1)
                a.activation(lnA[:, 5 * g5:5 * g5 + 5, :], banks[H2B[g5]][:, 0:5 * HALF].rearrange("p (a c) -> p a c", c=HALF)[:, :, 0:F],
                             ACT.Copy).then_inc(s.nc_a, 1)
            act.wait_ge(s.nc_v, NC_DEG)
            act.dma_start(lwt[:, 0:4], lw.rearrange("(o k) -> o k", o=1).to_broadcast([P, 4])).then_inc(s.ld_lw, 16)
            a.activation(nsc[:, 7:9, :], nsc[:, 4:6, :], ACT.Sqrt).then_inc(s.nc_a, 1)
            norm(s.nc_v, NC_LEAKY + 3, lnA, lnB, lnS, s.nc_a)
            norm(s.nc_v, NC_LEAKY + 13, lnA, lnB, lnS, s.nc_a)
            act.wait_ge(s.nd_v, 3)
            a.activation(lwt[:, 6:10], lwt[:, 0:4], ACT.Exp, bias=lwt[:, 5:6]).then_inc(s.nd_a, 1)

            def product(k):
                for t_, c in enumerate(CORDER):
                    act.wait_ge(s.acc_t, NPOS * k + t_ + 1)
                    if t_ >= 3:
                        act.wait_ge(s.out_t, NPOS * k + t_ - 2)
                    if c < NCH:
                        a.activation(accS[:, t_ % 3, :], banks[t_ % 4][:, :], ACT.Copy).then_inc(s.acc_c, 1)
                    else:
                        a.activation(accL[:, 0:LASTW], banks[t_ % 4][:, 0:LASTW], ACT.Copy).then_inc(s.acc_c, 1)
            for k in range(K2):
                product(k)
            act.wait_ge(s.comb_v, NPOS * K2)
            a.activation(gb, comb, ACT.Square).then_inc(s.nd_a, 1)
            act.wait_ge(s.nd_v, ND_DOUT)
            a.activation(nsc[:, 9, :], nsc[:, 6, :], ACT.Sqrt).then_inc(s.nd_a, 1)
            act.wait_ge(s.nd_v, ND_DOUT + 4)
            a.activation(nsc[:, 1, :], nsc[:, 0, :], ACT.Sqrt).then_inc(s.nd_a, 1)
            norm(s.nd_v, ND_LN2 + 3, comb, gb, nsc, s.nd_a)
            with act.Fori(0, (K3 - 2) // 2) as kk:
                for par in range(2):
                    product(2 * kk + (K2 + par))
            product(KTOT - 2)
            product(KTOT - 1)
            norm(s.nd_v, ND_LN3 + 3, comb, gb, nsc, s.nd_a)

        @block.tensor
        def _(pe):
            t = nc.tensor
            start_rings(pe, [s.pair_t, s.gen_mm] + [x for r in R for x in (r.pre, r.tr, r.seg, r.m_mm)])
            pe.wait_ge(s.consts, C_ALL)
            pe.wait_ge(s.ld_x, 16)
            for g4 in range(7):
                if g4 >= 2:
                    pe.wait_ge(s.xt_c, g4 - 1)
                for n in range(4 * g4, min(4 * g4 + 4, NB)):
                    last = t.transpose(banks[6 + g4 % 2][0:F, P * (n % 4):P * (n % 4) + P], xa[:, n, :], ident)
                last.then_inc(s.xt_t, 1)
            pe.wait_ge(s.ld_wts, WTS)
            for g4 in range(7):
                pe.wait_ge(s.xt_c, g4 + 1)
                if g4 >= 2:
                    pe.wait_ge(s.pq_c, g4 - 1)
                for n in range(4 * g4, min(4 * g4 + 4, NB)):
                    last = t.matmul(banks[2 + g4 % 2][:, P * (n % 4):P * (n % 4) + P], xT[0:F + 1, P * n:P * n + P],
                                    w1ab[0:F + 1, :], start=True, stop=True)
                last.then_inc(s.pq_t, 1)
            pe.wait_ge(s.prep_v, V_FLD)
            for j in range(8):
                if j >= 2:
                    pe.wait_ge(s.rec_c, j - 1)
                for f in range(4):
                    last = t.transpose(banks[j % 2][:, NSB * f:NSB * f + NSB], fld[f][:, P * j:P * j + P], ident[0:NSB, 0:NSB])
                last.then_inc(s.rec_t, 1)

            def transposes(r, h, b):
                hp, bp = (h, 1) if b == 0 else (h + 1, 0)
                if r is R[0]:
                    pe.wait_ge(r.oh[b], 2 * h + 2)
                    for j in range(4):
                        last = t.transpose(psT[0:2 * (SPAN + 1), P * j:P * j + P],
                                           OH[:, b, 2 * j:2 * j + 2, :].rearrange("p k c -> p (k c)"), ident)
                else:
                    pe.wait_ge(r.ea[b], 16 * (h + 1))
                    for j in range(2):
                        last = t.transpose(psT[:, P * j:P * j + P], EA[:, b, P * j:P * j + P], ident)
                last.then_inc(r.tr[b], 1)

            def products(r, h, b):
                pe.wait_ge(r.trc[b], h + 1)
                pe.wait_ge(r.add[b], h + 1)
                if r is R[0]:
                    pe.wait_ge(r.qd[b], 32 * (h + 1))
                    for j in range(4):
                        last = t.matmul(psPre[b][:, P * j:P * j + P], OHT[:, b, P * j:P * j + P], QD[:, b, :], start=True, stop=True)
                else:
                    for j in range(2):
                        last = t.matmul(psPre[b][:, 2 * P * j:2 * P * j + 2 * P], EAT[:, b, P * j:P * j + P], WEBD, start=True, stop=True)
                last.then_inc(r.pre[b], 1)

            def superblock(r, i, h, b, k, kh, q, mb, qh, more):
                hn, bn = following(h, b)
                if more:
                    pe.wait_ge(r.trc[b], h + 1)
                    transposes(r, hn, bn)
                pe.wait_ge(r.relu[b], h + 1)
                pe.wait_ge(r.oh[b], 2 * h + 2)
                pe.wait_ge(r.agg[b], h + 1)
                for j in range(8):
                    beside = ones if r is R[0] else OH[:, b, j, SPAN:SPAN + 1]
                    t.matmul(psSeg[0:F, P * b:P * b + SPAN], G[:, b, j, :], OH[:, b, j, 0:SPAN], start=j == 0, stop=j == 7)
                    last = t.matmul(psSeg[F:P, P * b:P * b + SPAN], beside.to_broadcast([P, F]), OH[:, b, j, 0:SPAN],
                                    start=j == 0, stop=j == 7)
                last.then_inc(r.seg[b], 1)
                if more:
                    products(r, hn, bn)
                if k is not None:
                    pe.wait_ge(s.pair_v[b], kh + 1 + 1)
                    pe.wait_ge(s.pair_e[b], 2 * kh + 1)
                    prod = psW[b].rearrange("p (c j) -> p c j", j=PAIR)
                    for w in range(2):
                        for j in range(TPW):
                            last = t.matmul(prod[:, :, WIN * w:WIN * w + WIN], alo[:, b, TPW * w + j, :],
                                            outer[:, b, TPW * w + j, :].rearrange("p (c j) -> p c j", j=WIN), start=j == 0, stop=j == TPW - 1)
                    last.then_inc(s.pair_t[b], 1)

            def ordered(layer):
                transposes(R[layer], 0, 0)
                products(R[layer], 0, 0)
                edge_loop(pe, layer, superblock)
                pe.wait_ge(R[layer].agg[0], NSB // 2 + 1 + 1)
                pe.wait_ge(R[layer].agg[1], NSB // 2 + 1)
                for b in range(2):
                    pe.wait_ge(s.pair_e[b], (NPAIR if layer else NLOOP) + 1)

            def gen_block(n, resident):
                pe.wait_ge(s.gen_out, (NCH + 1) * n + 1)

                def tiles(h, first, last_):
                    for b in range(2):
                        pe.wait_ge(s.gen_op[b], NT * n + 2 * h + 2)
                        for c in range(NCH + 1):
                            w_ = CH if c < NCH else LASTW
                            last = t.matmul(banks[c][:, 0:w_], genA[b], genB[b][:, CH * c:CH * c + w_],
                                            start=first and b == 0, stop=last_ and b == 1)
                        last.then_inc(s.gen_mm[b], 1)
                tiles(0, True, False)
                with pe.Fori(1, NT // 2 - 1) as h:
                    tiles(h, False, False)
                tiles(NT // 2 - 1, False, True)

            def general(r):
                with pe.Fori(0, NSB) as i:
                    if r is R[1]:
                        pe.wait_ge(r.m_ld, 48 * (i + 1))
                        for j in range(2):
                            last = t.transpose(psT[:, P * j:P * j + P], EA[:, 0, P * j:P * j + P], ident)
                        last.then_inc(r.m_tr, 1)
                        pe.wait_ge(r.m_trc, i + 1)
                        for j in range(2):
                            last = t.matmul(psPre[0][:, 2 * P * j:2 * P * j + 2 * P], EAT[:, 0, P * j:P * j + P], WEBD, start=True, stop=True)
                        last.then_inc(r.m_pre, 1)
                    pe.wait_ge(r.m_msg, i + 1)
                    pe.nop(nofuse=True)

                    def chunk(c, w_):
                        pe.wait_ge(r.m_agg, (NCH + 1) * i + c + 1)
                        for k in range(8):
                            pe.wait_ge(r.m_oh[k % 2], 4 * (NCH + 1) * i + 4 * c + (k // 2 + 1))
                            beside = ones if r is R[0] else wcol[:, k:k + 1]
                            t.matmul(psSeg[0:F, 0:w_], G[:, 0, k, :], genOH[k % 2][:, 0:w_], start=k == 0, stop=k == 7)
                            t.matmul(psSeg[F:P, 0:w_], beside.to_broadcast([P, F]), genOH[k % 2][:, 0:w_],
                                     start=k == 0, stop=k == 7).then_inc(r.m_mm[k % 2], 1)
                    chunks(pe, chunk)
                pe.wait_ge(r.m_agg, (NCH + 1) * NSB + 1)

            def general0():
                pe.wait_ge(s.pq_c, 7)
                pe.wait_ge(s.rec_c, 8)
                blocks(pe, gen_block)
                pe.wait_ge(s.gen_out, (NCH + 1) * NB + 1)
                general(R[0])

            pe.wait_ge(s.flag, 1)
            by_order(pe, general0, lambda: ordered(0))
            for g5 in range(5):
                for n in range(5):
                    lo_ = P * (5 * g5 + n)
                    last = t.matmul(banks[g5][:, HALF * n:HALF * n + HALF], aggT[0:F + 1, lo_:lo_ + P], w2p[0:F + 1, :], start=True, stop=True)
                last.then_inc(s.nb_t, 1)
            pe.wait_ge(s.nb_v, NB_Y)
            pe.wait_ge(s.ld_we, 4 * 16)
            by_order(pe, lambda: general(R[1]), lambda: ordered(1))
            for g4 in range(7):
                for n in range(4 * g4, min(4 * g4 + 4, NB)):
                    last = t.transpose(banks[g4][0:F, P * (n % 4):P * (n % 4) + P], xa[:, n, :], ident)
                last.then_inc(s.nc_t, 1)
            pe.wait_ge(s.nc_v, NC_HT)
            for g4 in range(7):
                w_ = min(CH, NP - CH * g4)
                t.matmul(banks[(4 + g4) % 7][0:F, 0:w_], w1n, hT[0:F, CH * g4:CH * g4 + w_], start=True, stop=True).then_inc(s.nc_t, 1)
            pe.wait_ge(s.nc_a, NCA_H1)
            for g5 in range(5):
                for n in range(5):
                    lo_ = P * (5 * g5 + n)
                    last = t.matmul(banks[H2B[g5]][:, HALF * n:HALF * n + HALF], h1T[0:F + 1, lo_:lo_ + P], w2n, start=True, stop=True)
                last.then_inc(s.nc_t, 1)
            pe.wait_ge(s.nc_a, NCA_H1 + 2)
            for g5 in range(5):
                for n in range(5):
                    lo_ = P * (5 * g5 + n)
                    last = t.matmul(banks[DEGB[g5]][:, HALF * n:HALF * n + HALF], aggT[:, lo_:lo_ + P], sel, start=True, stop=True)
                last.then_inc(s.nc_t, 1)

            def turn_chunk(k, t_):
                pe.wait_ge(s.acc_c, NPOS * k + t_ + 1)
                if t_ >= 4 or t_ < 0:
                    pe.wait_ge(s.xs_v, NPOS * k + t_ - 3)
                slot = t_ % NPOS
                c = CORDER[slot]
                for n in range(4 if c < NCH else 1):
                    left = accS[:, slot % 3, P * n:P * n + P] if c < NCH else accL
                    last = t.transpose(banks[4 + slot % 4][:, P * n:P * n + P], left, ident)
                last.then_inc(s.out_t, 1)

            def product(k, old, first=False, last_=False):
                if not first:
                    pe.wait_ge(s.xs_v, NPOS * k - 1)
                for t_, c in enumerate(CORDER):
                    w_ = CH if c < NCH else LASTW
                    if t_ >= 4:
                        pe.wait_ge(s.acc_c, NPOS * k + t_ - 3)
                    for n in range(NB):
                        piece = NPC * c + (n - RES) // PIECE
                        if n == 20 and t_ == 0 and not first:
                            pe.wait_ge(s.xs_v, NPOS * k)
                        if n < RES:
                            right = Wres[:, n, CH * c:CH * c + w_]
                        elif c == NCH:
                            right = W6[:, n - RES, :]
                        else:
                            if (n - RES) % PIECE == 0:
                                pe.wait_ge(s.pc[piece % RING], 16 * (NPIECE // RING * k + piece // RING + 1))
                            right = ring[:, piece % RING, :].rearrange("p (q a e) -> p a q e", q=CH // QC, e=QC)[:, (n - RES) % PIECE, :, :]
                        last = t.matmul(banks[t_ % 4][F * (n % 2):F * (n % 2) + F, 0:w_], old[:, n, :], right, start=n < 2, stop=n >= NB - 2)
                        if c < NCH and n < NB - 1 and n >= RES and (n - RES) % PIECE == PIECE - 1:
                            last.then_inc(s.pc_free, 1)
                        if n == (RES - 1 if t_ else TURN_AT) and not (t_ == 0 and first):
                            turn_chunk(k, t_ - 1)
                    last.then_inc(s.acc_t, 1)
                if last_:
                    turn_chunk(k, NPOS - 1)

            pe.wait_ge(s.nd_v, 1)
            for k in range(K2):
                product(k, xs[k % 2], k == 0, k == K2 - 1)
            pe.wait_ge(s.nd_v, ND_L3)
            product(K2, xs[1], True)
            with pe.Fori(0, (K3 - 2) // 2) as kk:
                for par in range(2):
                    product(2 * kk + (K2 + 1 + par), xs[par])
            product(KTOT - 1, xs[0], False, True)


_INS = ["x", "src", "dst", "edge_attr_32", "edge_weight", "edge_weight1", "L0_gnn_W1", "L0_gnn_b1",
        "L0_gnn_W2", "L0_gnn_b2", "L1_gnn_We", "L1_gnn_be", "L1_gnn_W1", "L1_gnn_b1", "L1_gnn_W2",
        "L1_gnn_b2", "L1_gnn_eps_gin", "L1_gnn_gamma", "L1_gnn_beta", "L2_gnn_layer_weights"]


def kernel(**inputs):
    import concourse.bacc as _bacc
    from concourse.bass_utils import run_bass_kernel_spmd as _run

    pads = {"x": (NP, 0), "src": (EP, 0), "dst": (EP, NP), "edge_attr_32": (EP, 0),
            "edge_weight": (EP, 0), "edge_weight1": (EP, 0)}
    nc = _bacc.Bacc("TRN2", target_bir_lowering=False, num_devices=1)
    arrays, args = {}, []
    for name in _INS:
        a = np.ascontiguousarray(inputs[name])
        if name == "edge_weight1":
            a = a.reshape(E)
        if name == "L1_gnn_eps_gin":
            a = a.reshape(1)
        if name in pads:
            rows, fill = pads[name]
            full = np.full((rows,) + a.shape[1:], fill, a.dtype)
            full[:a.shape[0]] = a
            a = full
        arrays[f"in_{name}"] = a
        args.append(nc.dram_tensor(f"in_{name}", a.shape, mybir.dt.from_np(a.dtype), kind="ExternalInput").ap())
    args.append(nc.dram_tensor("out_0", (N, F), mybir.dt.float32, kind="ExternalOutput").ap())
    build(nc, *args)
    return _run(nc, [arrays], core_ids=[0]).results[0]["out_0"]
```
